# Optimizing a Trainium2 kernel written in Bass

```python
import numpy as np
import jax
import jax.numpy as jnp

def _softmax(x, axis=-1):
    return jax.nn.softmax(x, axis=axis)

def _gelu(x):
    return jax.nn.gelu(x, approximate=True)

def _silu(x):
    return jax.nn.silu(x)

def _sigmoid(x):
    return jax.nn.sigmoid(x)

def _layernorm(x, axis=-1, eps=1e-05):
    m = jnp.mean(x, axis=axis, keepdims=True)
    v = jnp.var(x, axis=axis, keepdims=True)
    return (x - m) / jnp.sqrt(v + eps)

def _scatter_add(tgt, idx, src, axis=0):
    return tgt.at[idx].add(src)

def _segment_sum(src, seg, n):
    return jax.ops.segment_sum(src, seg, n)
kernel_name = 'mk_adaln_attn_ffn_d1_seqx_r8_00331e'

def setup_inputs(seed: int=0):
    np.random.seed(seed)
    _w = jnp.asarray

    def _rec_inputs():
        import jax
        import jax.numpy as jnp
        _rk = jax.random.key(seed)
        x = -0.000125 + 0.9999 * jax.random.normal(jax.random.fold_in(_rk, 1), (32, 128, 128), jnp.float32)
        _lenS = 128 - jax.random.randint(jax.random.fold_in(_rk, 7), (32,), 0, max(1, 128 // 4) + 1, jnp.int32)
        _lenS2 = 128 - jax.random.randint(jax.random.fold_in(_rk, 8), (32,), 0, max(1, 128 // 4) + 1, jnp.int32)
        condB_deltat = jax.random.uniform(jax.random.fold_in(_rk, 11), (32,), jnp.float32, 0.0, 1.99976)
        itok_B_0_7 = jax.random.randint(jax.random.fold_in(_rk, 12), (32,), 0, 8, jnp.int32)
        return (x, condB_deltat, itok_B_0_7)
    x, condB_deltat, itok_B_0_7 = _rec_inputs()

    def _L0_cond_setup():
        import jax, jax.numpy as jnp
        import numpy as np
        B, F, T = (32, 64, 128)
        key = jax.random.key(seed)
        k1, k2, k3, k4 = jax.random.split(key, 4)
        x = jax.random.normal(k1, (B, 2 * F, T), dtype=jnp.float32)
        delta_t = jax.random.uniform(k2, (B,), dtype=jnp.float32, minval=0.5, maxval=2.0)
        amplitudes = jax.random.uniform(k3, (F,), dtype=jnp.float32, minval=0.7, maxval=1.3)
        frequencies = jax.random.uniform(k4, (F,), dtype=jnp.float32, minval=0.0, maxval=2.0 * np.pi)
        return {'x': x, 'delta_t': delta_t, 'amplitudes': amplitudes, 'frequencies': frequencies}
    _L0_cond_all = _L0_cond_setup()
    _L0_cond_in = {k: v for k, v in _L0_cond_all.items() if k in ('amplitudes', 'frequencies')}
    del _L0_cond_all

    def _L0_attn_setup():
        import jax, jax.numpy as jnp
        import numpy as np
        from jax import lax
        H = 128
        DI = 256
        N = 16
        DC = 4
        DTR = 64
        B, L = (2, 256)
        EPS = 1e-05

        def _selective_scan(u, delta, A, Bm, Cm, D):

            def step(h, inp):
                d, b, c, ut = inp
                dA = jnp.exp(d[:, :, None] * A)
                h = dA * h + (d * ut)[:, :, None] * b[:, None, :]
                y = jnp.einsum('bdn,bn->bd', h, c)
                return (h, y)
            h0 = jnp.zeros((u.shape[0], A.shape[0], A.shape[1]), u.dtype)
            xs = (delta.transpose(1, 0, 2), Bm.transpose(1, 0, 2), Cm.transpose(1, 0, 2), u.transpose(1, 0, 2))
            _, ys = lax.scan(step, h0, xs)
            return ys.transpose(1, 0, 2) + u * D

        def _mamba(x, in_proj_w, conv_w, conv_b, x_proj_w, dt_proj_w, dt_proj_b, A_log, D, out_proj_w):
            xz = x @ in_proj_w.T
            xi, z = (xz[..., :DI], xz[..., DI:])
            xc = lax.conv_general_dilated(xi.transpose(0, 2, 1), conv_w, window_strides=(1,), padding=[(DC - 1, 0)], feature_group_count=DI) + conv_b[None, :, None]
            xi = jax.nn.silu(xc.transpose(0, 2, 1))
            dbc = xi @ x_proj_w.T
            dt, Bm, Cm = (dbc[..., :DTR], dbc[..., DTR:DTR + N], dbc[..., DTR + N:])
            delta = jax.nn.softplus(dt @ dt_proj_w.T + dt_proj_b)
            A = -jnp.exp(A_log)
            y = _selective_scan(xi, delta, A, Bm, Cm, D)
            y = y * jax.nn.silu(z)
            return y @ out_proj_w.T
        key = jax.random.key(seed)
        ks = jax.random.split(key, 12)
        rn = lambda k, shp, sc=0.02: jax.random.normal(k, shp, jnp.float32) * sc
        return {'x': jax.random.normal(ks[0], (B, L, H), jnp.float32), 'ln_g': jnp.ones((H,), jnp.float32), 'ln_b': jnp.zeros((H,), jnp.float32), 'in_proj_w': rn(ks[1], (2 * DI, H)), 'conv_w': rn(ks[2], (DI, 1, DC), 0.2), 'conv_b': jnp.zeros((DI,), jnp.float32), 'x_proj_w': rn(ks[3], (DTR + 2 * N, DI)), 'dt_proj_w': rn(ks[4], (DI, DTR), 0.1), 'dt_proj_b': jax.random.uniform(ks[5], (DI,), jnp.float32, -4.0, -2.0), 'A_log': jnp.tile(jnp.log(jnp.arange(1, N + 1, dtype=jnp.float32))[None, :], (DI, 1)), 'D': jnp.ones((DI,), jnp.float32), 'out_proj_w': rn(ks[6], (H, DI)), 'dim_reduce_w': rn(ks[7], (H, 2 * H)), 'dim_reduce_b': jnp.zeros((H,), jnp.float32), 'glu_w': rn(ks[8], (2 * H, H)), 'glu_b': jnp.zeros((2 * H,), jnp.float32)}
    _L0_attn_all = _L0_attn_setup()
    _L0_attn_in = {k: v for k, v in _L0_attn_all.items() if k in ('ln_g', 'ln_b', 'in_proj_w', 'conv_w', 'conv_b', 'x_proj_w', 'dt_proj_w', 'dt_proj_b', 'A_log', 'D', 'out_proj_w', 'dim_reduce_w', 'dim_reduce_b', 'glu_w', 'glu_b')}
    del _L0_attn_all

    def _L0_cond2_setup():
        import jax, jax.numpy as jnp
        import numpy as np
        B, S, D, F = (32, 64, 128, 512)
        R_COMMON, R_DOMAIN, E = (16, 16, 8)
        ALPHA = 2.0

        def _expert_lora(x, expert_ids, Wa, Wb):
            Ab = Wa[expert_ids]
            Bb = Wb[expert_ids]
            low = jnp.einsum('bsd,brd->bsr', x, Ab)
            return ALPHA * jnp.einsum('bsr,bor->bso', low, Bb)
        key = jax.random.key(seed)
        ks = jax.random.split(key, 12)
        sd = lambda k, shape: jax.random.normal(k, shape, dtype=jnp.float32) * (1.0 / np.sqrt(shape[-1]))
        return {'hidden_states': jax.random.normal(ks[0], (B, S, D), dtype=jnp.float32), 'expert_ids': jax.random.randint(ks[1], (B,), 0, E, dtype=jnp.int32), 'wi': sd(ks[2], (F, D)), 'wo': sd(ks[3], (D, F)), 'common_wi_a': sd(ks[4], (R_COMMON, D)), 'common_wi_b': sd(ks[5], (F, R_COMMON)), 'common_wo_a': sd(ks[6], (R_COMMON, F)), 'common_wo_b': sd(ks[7], (D, R_COMMON)), 'experts_wi_a': sd(ks[8], (E, R_DOMAIN, D)), 'experts_wi_b': sd(ks[9], (F, R_DOMAIN)) * jnp.ones((E, 1, 1)) * 0.0 + sd(ks[9], (E, F, R_DOMAIN)), 'experts_wo_a': sd(ks[10], (E, R_DOMAIN, F)), 'experts_wo_b': sd(ks[11], (E, D, R_DOMAIN))}
    _L0_cond2_all = _L0_cond2_setup()
    _L0_cond2_in = {k: v for k, v in _L0_cond2_all.items() if k in ('wi', 'wo', 'common_wi_a', 'common_wi_b', 'common_wo_a', 'common_wo_b', 'experts_wi_a', 'experts_wi_b', 'experts_wo_a', 'experts_wo_b')}
    del _L0_cond2_all

    def _L0_ffn_setup():
        import jax, jax.numpy as jnp
        import numpy as np
        D_IN, D_HID = (128, 512)

        def _ternary(key, shape):
            return jax.random.randint(key, shape, -1, 2).astype(jnp.float32)

        def _tlin(x, w, s):
            return jnp.einsum('bsi,oi->bso', x, w) * s
        key = jax.random.key(seed)
        ks = jax.random.split(key, 12)
        inv = lambda fan: 1.0 / np.sqrt(fan).astype(np.float32)
        return {'x': jax.random.normal(ks[0], (4, 256, D_IN), dtype=jnp.float32), 'w1_w': _ternary(ks[1], (D_HID, D_IN)), 'w1_s': jax.random.uniform(ks[2], (D_HID,), dtype=jnp.float32) * inv(D_IN), 'w2_w': _ternary(ks[3], (D_HID, D_IN)), 'w2_s': jax.random.uniform(ks[4], (D_HID,), dtype=jnp.float32) * inv(D_IN), 'h1_w': _ternary(ks[5], (D_HID, D_HID)), 'h1_s': jax.random.uniform(ks[6], (D_HID,), dtype=jnp.float32) * inv(D_HID), 'h2_w': _ternary(ks[7], (D_HID, D_HID)), 'h2_s': jax.random.uniform(ks[8], (D_HID,), dtype=jnp.float32) * inv(D_HID), 'w3_w': _ternary(ks[9], (D_IN, D_HID)), 'w3_s': jax.random.uniform(ks[10], (D_IN,), dtype=jnp.float32) * inv(D_HID)}
    _L0_ffn_all = _L0_ffn_setup()
    _L0_ffn_in = {k: v for k, v in _L0_ffn_all.items() if k in ('w1_w', 'w1_s', 'w2_w', 'w2_s', 'h1_w', 'h1_s', 'h2_w', 'h2_s', 'w3_w', 'w3_s')}
    del _L0_ffn_all
    return {'x': x, 'condB_deltat': condB_deltat, 'itok_B_0_7': itok_B_0_7, 'L0_cond_amplitudes': _L0_cond_in['amplitudes'], 'L0_cond_frequencies': _L0_cond_in['frequencies'], 'L0_attn_ln_g': _L0_attn_in['ln_g'], 'L0_attn_ln_b': _L0_attn_in['ln_b'], 'L0_attn_in_proj_w': _L0_attn_in['in_proj_w'], 'L0_attn_conv_w': _L0_attn_in['conv_w'], 'L0_attn_conv_b': _L0_attn_in['conv_b'], 'L0_attn_x_proj_w': _L0_attn_in['x_proj_w'], 'L0_attn_dt_proj_w': _L0_attn_in['dt_proj_w'], 'L0_attn_dt_proj_b': _L0_attn_in['dt_proj_b'], 'L0_attn_A_log': _L0_attn_in['A_log'], 'L0_attn_D': _L0_attn_in['D'], 'L0_attn_out_proj_w': _L0_attn_in['out_proj_w'], 'L0_attn_dim_reduce_w': _L0_attn_in['dim_reduce_w'], 'L0_attn_dim_reduce_b': _L0_attn_in['dim_reduce_b'], 'L0_attn_glu_w': _L0_attn_in['glu_w'], 'L0_attn_glu_b': _L0_attn_in['glu_b'], 'L0_cond2_wi': _L0_cond2_in['wi'], 'L0_cond2_wo': _L0_cond2_in['wo'], 'L0_cond2_common_wi_a': _L0_cond2_in['common_wi_a'], 'L0_cond2_common_wi_b': _L0_cond2_in['common_wi_b'], 'L0_cond2_common_wo_a': _L0_cond2_in['common_wo_a'], 'L0_cond2_common_wo_b': _L0_cond2_in['common_wo_b'], 'L0_cond2_experts_wi_a': _L0_cond2_in['experts_wi_a'], 'L0_cond2_experts_wi_b': _L0_cond2_in['experts_wi_b'], 'L0_cond2_experts_wo_a': _L0_cond2_in['experts_wo_a'], 'L0_cond2_experts_wo_b': _L0_cond2_in['experts_wo_b'], 'L0_ffn_w1_w': _L0_ffn_in['w1_w'], 'L0_ffn_w1_s': _L0_ffn_in['w1_s'], 'L0_ffn_w2_w': _L0_ffn_in['w2_w'], 'L0_ffn_w2_s': _L0_ffn_in['w2_s'], 'L0_ffn_h1_w': _L0_ffn_in['h1_w'], 'L0_ffn_h1_s': _L0_ffn_in['h1_s'], 'L0_ffn_h2_w': _L0_ffn_in['h2_w'], 'L0_ffn_h2_s': _L0_ffn_in['h2_s'], 'L0_ffn_w3_w': _L0_ffn_in['w3_w'], 'L0_ffn_w3_s': _L0_ffn_in['w3_s']}

def reference(x, condB_deltat, itok_B_0_7, L0_cond_amplitudes, L0_cond_frequencies, L0_attn_ln_g, L0_attn_ln_b, L0_attn_in_proj_w, L0_attn_conv_w, L0_attn_conv_b, L0_attn_x_proj_w, L0_attn_dt_proj_w, L0_attn_dt_proj_b, L0_attn_A_log, L0_attn_D, L0_attn_out_proj_w, L0_attn_dim_reduce_w, L0_attn_dim_reduce_b, L0_attn_glu_w, L0_attn_glu_b, L0_cond2_wi, L0_cond2_wo, L0_cond2_common_wi_a, L0_cond2_common_wi_b, L0_cond2_common_wo_a, L0_cond2_common_wo_b, L0_cond2_experts_wi_a, L0_cond2_experts_wi_b, L0_cond2_experts_wo_a, L0_cond2_experts_wo_b, L0_ffn_w1_w, L0_ffn_w1_s, L0_ffn_w2_w, L0_ffn_w2_s, L0_ffn_h1_w, L0_ffn_h1_s, L0_ffn_h2_w, L0_ffn_h2_s, L0_ffn_w3_w, L0_ffn_w3_s):
    import jax
    import jax.numpy as jnp

    def _L0_cond_ref(x, delta_t, amplitudes, frequencies):
        import jax, jax.numpy as jnp
        import numpy as np
        B, F, T = (32, 64, 128)
        Bn = x.shape[0]
        Fn = amplitudes.shape[0]
        a = amplitudes[None, :] ** delta_t[:, None]
        ang = frequencies[None, :] * delta_t[:, None]
        c = a * jnp.cos(ang)
        s = a * jnp.sin(ang)
        xr = x.reshape(Bn, Fn, 2, -1)
        x0, x1 = (xr[:, :, 0], xr[:, :, 1])
        out0 = c[..., None] * x0 - s[..., None] * x1
        out1 = s[..., None] * x0 + c[..., None] * x1
        return jnp.stack([out0, out1], axis=2).reshape(x.shape)

    def _L0_attn_ref(x, ln_g, ln_b, in_proj_w, conv_w, conv_b, x_proj_w, dt_proj_w, dt_proj_b, A_log, D, out_proj_w, dim_reduce_w, dim_reduce_b, glu_w, glu_b):
        import jax, jax.numpy as jnp
        import numpy as np
        from jax import lax
        H = 128
        DI = 256
        N = 16
        DC = 4
        DTR = 64
        B, L = (2, 256)
        EPS = 1e-05

        def _selective_scan(u, delta, A, Bm, Cm, D):

            def step(h, inp):
                d, b, c, ut = inp
                dA = jnp.exp(d[:, :, None] * A)
                h = dA * h + (d * ut)[:, :, None] * b[:, None, :]
                y = jnp.einsum('bdn,bn->bd', h, c)
                return (h, y)
            h0 = jnp.zeros((u.shape[0], A.shape[0], A.shape[1]), u.dtype)
            xs = (delta.transpose(1, 0, 2), Bm.transpose(1, 0, 2), Cm.transpose(1, 0, 2), u.transpose(1, 0, 2))
            _, ys = lax.scan(step, h0, xs)
            return ys.transpose(1, 0, 2) + u * D

        def _mamba(x, in_proj_w, conv_w, conv_b, x_proj_w, dt_proj_w, dt_proj_b, A_log, D, out_proj_w):
            xz = x @ in_proj_w.T
            xi, z = (xz[..., :DI], xz[..., DI:])
            xc = lax.conv_general_dilated(xi.transpose(0, 2, 1), conv_w, window_strides=(1,), padding=[(DC - 1, 0)], feature_group_count=DI) + conv_b[None, :, None]
            xi = jax.nn.silu(xc.transpose(0, 2, 1))
            dbc = xi @ x_proj_w.T
            dt, Bm, Cm = (dbc[..., :DTR], dbc[..., DTR:DTR + N], dbc[..., DTR + N:])
            delta = jax.nn.softplus(dt @ dt_proj_w.T + dt_proj_b)
            A = -jnp.exp(A_log)
            y = _selective_scan(xi, delta, A, Bm, Cm, D)
            y = y * jax.nn.silu(z)
            return y @ out_proj_w.T
        skip = x
        mu = x.mean(-1, keepdims=True)
        var = ((x - mu) ** 2).mean(-1, keepdims=True)
        xn = (x - mu) * lax.rsqrt(var + EPS) * ln_g + ln_b
        margs = (in_proj_w, conv_w, conv_b, x_proj_w, dt_proj_w, dt_proj_b, A_log, D, out_proj_w)
        x_f = _mamba(xn, *margs)
        x_r = jnp.flip(_mamba(jnp.flip(xn, 1), *margs), 1)
        y = jnp.concatenate([x_f, x_r], axis=-1) @ dim_reduce_w.T + dim_reduce_b
        y = jax.nn.gelu(y, approximate=False)
        g = y @ glu_w.T + glu_b
        y = g[..., :H] * jax.nn.sigmoid(g[..., H:])
        return y + skip

    def _L0_cond2_ref(hidden_states, expert_ids, wi, wo, common_wi_a, common_wi_b, common_wo_a, common_wo_b, experts_wi_a, experts_wi_b, experts_wo_a, experts_wo_b):
        import jax, jax.numpy as jnp
        import numpy as np
        B, S, D, F = (32, 64, 128, 512)
        R_COMMON, R_DOMAIN, E = (16, 16, 8)
        ALPHA = 2.0

        def _expert_lora(x, expert_ids, Wa, Wb):
            Ab = Wa[expert_ids]
            Bb = Wb[expert_ids]
            low = jnp.einsum('bsd,brd->bsr', x, Ab)
            return ALPHA * jnp.einsum('bsr,bor->bso', low, Bb)
        x = hidden_states
        hidden_i = jnp.einsum('bsd,fd->bsf', x, wi)
        hidden_i += ALPHA * jnp.einsum('bsr,fr->bsf', jnp.einsum('bsd,rd->bsr', x, common_wi_a), common_wi_b)
        hidden_i += _expert_lora(x, expert_ids, experts_wi_a, experts_wi_b)
        hidden_i = jax.nn.relu(hidden_i)
        hidden_o = jnp.einsum('bsf,df->bsd', hidden_i, wo)
        hidden_o += ALPHA * jnp.einsum('bsr,dr->bsd', jnp.einsum('bsf,rf->bsr', hidden_i, common_wo_a), common_wo_b)
        hidden_o += _expert_lora(hidden_i, expert_ids, experts_wo_a, experts_wo_b)
        return hidden_o

    def _L0_ffn_ref(x, w1_w, w1_s, w2_w, w2_s, h1_w, h1_s, h2_w, h2_s, w3_w, w3_s):
        import jax, jax.numpy as jnp
        import numpy as np
        D_IN, D_HID = (128, 512)

        def _ternary(key, shape):
            return jax.random.randint(key, shape, -1, 2).astype(jnp.float32)

        def _tlin(x, w, s):
            return jnp.einsum('bsi,oi->bso', x, w) * s
        h = jax.nn.silu(_tlin(x, w1_w, w1_s)) * _tlin(x, w2_w, w2_s)
        h = jax.nn.gelu(_tlin(h, h1_w, h1_s), approximate=False)
        h = jax.nn.gelu(_tlin(h, h2_w, h2_s), approximate=False)
        return _tlin(h, w3_w, w3_s)
    x = x + _L0_attn_ref(_L0_cond_ref(x, condB_deltat, L0_cond_amplitudes, L0_cond_frequencies), L0_attn_ln_g, L0_attn_ln_b, L0_attn_in_proj_w, L0_attn_conv_w, L0_attn_conv_b, L0_attn_x_proj_w, L0_attn_dt_proj_w, L0_attn_dt_proj_b, L0_attn_A_log, L0_attn_D, L0_attn_out_proj_w, L0_attn_dim_reduce_w, L0_attn_dim_reduce_b, L0_attn_glu_w, L0_attn_glu_b)
    x = x + _L0_ffn_ref(_L0_cond2_ref(x, itok_B_0_7, L0_cond2_wi, L0_cond2_wo, L0_cond2_common_wi_a, L0_cond2_common_wi_b, L0_cond2_common_wo_a, L0_cond2_common_wo_b, L0_cond2_experts_wi_a, L0_cond2_experts_wi_b, L0_cond2_experts_wo_a, L0_cond2_experts_wo_b), L0_ffn_w1_w, L0_ffn_w1_s, L0_ffn_w2_w, L0_ffn_w2_s, L0_ffn_h1_w, L0_ffn_h1_s, L0_ffn_h2_w, L0_ffn_h2_s, L0_ffn_w3_w, L0_ffn_w3_s)
    return x

_drawn_inputs = setup_inputs


def setup_inputs(seed=0):
    import zlib

    import numpy as np

    out = dict(_drawn_inputs(seed))
    spreads = {'L0_attn_ln_g': (1.0, 0.2),
     'L0_attn_ln_b': (0.0, 0.1),
     'L0_attn_conv_b': (0.0, 0.1),
     'L0_attn_D': (1.0, 0.2),
     'L0_attn_dim_reduce_b': (0.0, 0.1),
     'L0_attn_glu_b': (0.0, 0.1)}
    factors = {}
    for name, (base, spread) in spreads.items():
        noise = np.random.default_rng([zlib.crc32(name.encode()), seed]).standard_normal(out[name].shape)
        drawn = base * np.exp(spread * noise) if base else spread * noise
        out[name] = jnp.asarray(drawn.astype(out[name].dtype))
    for name, factor in factors.items():
        out[name] = (out[name] * factor).astype(out[name].dtype)
    return out
```

```python
from collections import namedtuple
from contextlib import ExitStack

import numpy as np

import concourse.bass as bass
from concourse import mybir

F32 = mybir.dt.float32
BF16 = mybir.dt.bfloat16
I32 = mybir.dt.int32
ALU = mybir.AluOpType
ACT = mybir.ActivationFunctionType

P = 128
BATCH, LEN, HID = 32, 128, 128
DI, NST, TAPS, DTR = 256, 16, 4, 64
EXPERTS, RANK, FF = 8, 16, 512
LN_EPS, LORA_ALPHA = 1e-5, 2.0

GS = 4
NG = BATCH // GS
GT = GS * LEN
HALVES = DI // P
FC = FF // P
UNITS = 2 * NST
RING = 8

COLS = {}
_at = 0
for _name, _n in (("conv_w", HALVES * TAPS), ("conv_b", HALVES), ("dt_b", HALVES), ("skip_d", HALVES),
                  ("a_log", HALVES * NST), ("ln_g", 1), ("ln_b", 1), ("reduce_b", 1), ("glu_b", 2),
                  ("w1_s", FC), ("w2_s", FC), ("h1_s", FC), ("h2_s", FC), ("w3_s", 1)):
    COLS[_name] = _at
    _at += _n
NCOLS = _at

(F_NORM, F_XI0, F_XI1, F_Z0, F_Z1, F_DBC0, F_DT00, F_DT01, F_DBC1, F_DT10, F_DT11) = range(11)
FRONT_FILLS = 11
B_OUT, B_GLU0, B_GLU1, B_RES = range(4)
B_HID, B_WO = 4, 8
B_GATE = (9, 10, 13, 14)
B_UP = (11, 12, 15, 16)
B_H1, B_H2, B_W3, B_TOK = 17, 21, 25, 26
BACK_FILLS = 27
BANK_FILLS = ((BACK_FILLS + 1) // 2, BACK_FILLS // 2)

POOL_PAIRS = (0, 2, 4, 6)
DVE_PAIRS = (1, 3, 5, 7)

Group = namedtuple("Group", "number parity turn")


def group(i, c):
    return Group(i * 2 + c, c % 2, i + c // 2)


def wait(eng, signal, value):
    if isinstance(value, int) and value <= 0:
        return
    eng.wait_ge(signal, value)


def build(nc, x, delta_t, expert_ids, amplitudes, frequencies, columns, w_in, w_x, w_dt, w_out, w_reduce, w_glu,
          wi, wo, common_wi_a, common_wi_b, common_wo_a, common_wo_b,
          experts_wi_a, experts_wi_b, experts_wo_a, experts_wo_b, w1, w2, h1, h2, w3, merged, out):
    PI = float(np.pi)
    ctx = ExitStack()
    with ctx:
        def sb(name, shape, dt=F32):
            return ctx.enter_context(nc.sbuf_tensor(name, shape, dt))

        def sem(name):
            return ctx.enter_context(nc.semaphore(name))

        col = sb("col", [P, NCOLS])
        w_in_s = sb("w_in_s", [P, 2 * DI])
        w_x_s = sb("w_x_s", [P, HALVES, DTR + 2 * NST])
        w_dt_s = sb("w_dt_s", [DTR, DI])
        w_fused = sb("w_fused", [P, 2, HALVES, HID])
        w_glu_s = sb("w_glu_s", [P, 2 * HID])
        w1_s = sb("w1_s", [P, FF])
        w2_s = sb("w2_s", [P, FF])
        h1_s = sb("h1_s", [P, FC, FF])
        h2_s = sb("h2_s", [P, FC, FF])
        w3_s = sb("w3_s", [P, FC, HID])
        ident = sb("ident", [P, P])
        pick = sb("pick", [96, 32], BF16)
        spread = sb("spread", [96, 32, P], BF16)
        a_neg = sb("a_neg", [P, HALVES, NST])
        hb = sb("hb", [P, 2])
        rot = sb("rot", [P, 8, BATCH // 2])
        half_power = sb("half_power", [P, GS])
        one_col = sb("one_col", [P, 1])
        halfpi_col = sb("halfpi_col", [P, 1])
        freq_amp = sb("freq_amp", [P, 2])

        xin = sb("xin", [P, 2, 2, 2, HID])
        scaled = sb("scaled", [P, 2, 2, HID])
        xc = sb("xc", [P, 2, 2, HID])
        xn = scaled
        stats = sb("stats", [P, GS, 6])
        moments = sb("moments", [P, GS, 2])
        var_eps = sb("var_eps", [P, GS])
        rstd = sb("rstd", [P, GS])
        resid = sb("resid", [P, 2, 2, 2, HID])
        xnT = sb("xnT", [P, GT])
        u_f = sb("u_f", [P, 2, HALVES, GT])
        u_r = sb("u_r", [P, 2, HALVES, GT])
        z = sb("z", [P, 2, HALVES, GT])
        dtT = sb("dtT", [DTR, GT])
        parts = sb("parts", [96, 2, GT], BF16)
        rest = sb("rest", [64, GT])
        relu_dt = sb("relu_dt", [P, HALVES, GT])
        acc_r = relu_dt
        log_dt = sb("log_dt", [P, HALVES, GT])
        delta = sb("delta", [P, 2, HALVES, GT])
        du = sb("du", [P, 2, HALVES, GT])

        decay = sb("decay", [P, 2, HALVES, GS, LEN])
        b_rows = sb("b_rows", [P, 2, GT])
        state = sb("state", [P, RING, HALVES, GT])

        ysum = sb("ysum", [P, HALVES, GT])
        gated = sb("gated", [P, 2, HALVES, GT])
        gy = sb("gy", [P, GT])
        glu_a = sb("glu_a", [P, GT])
        glu_t = sb("glu_t", [P, GT])
        x1T = sb("x1T", [P, GT])
        wsel = sb("wsel", [P, GS, 2 * FF])
        hidA = sb("hidA", [P, FC, GT])
        hidB = sb("hidB", [P, FC, GT])
        cT = glu_a
        gate = sb("gate", [P, 2, GT])
        w_out_s = gate[:, 0, 0:DI]
        w_reduce_s = gate[:, 1, 0:2 * HID].rearrange("p (d o) -> p d o", d=2)
        oT = glu_t
        tok = gy

        bank_b = ctx.enter_context(nc.psum_tensor("bank_b", [P, GT], F32))
        bank_c = [ctx.enter_context(nc.psum_tensor(f"bank_c{i}", [P, GT], F32)) for i in range(2)]
        bank_y = ctx.enter_context(nc.psum_tensor("bank_y", [P, HALVES, GT], F32))
        bank_f = ctx.enter_context(nc.psum_tensor("bank_f", [P, GT], F32))
        bank_k = [ctx.enter_context(nc.psum_tensor(f"bank_k{i}", [P, GT], F32)) for i in range(2)]

        names = """small_loaded front_w_loaded fuse_w_loaded back_w_loaded lora_loaded0 lora_loaded1 base_loaded
            ident_ready pick_zero pick_step spread_ready consts_ready decay_zero rot_act rot_dve rot_ready a_ready
            hb_ready fused_full fused_ready lora_full lora_merged0 lora_merged1 lora_stored0 lora_stored1
            x_loaded0 x_loaded1 scaled_ready cond_done stats_done aggr_done var_ready rstd_ready xn_ready resid_ready
            front_full front_taken conv_init conv_tap u_ready dt_copied rest_ready mid_ready parts_ready
            relu_ready abs_ready exp_ready log_ready delta_ready du_ready
            b_full b_copied c_full exp_done bx_ready scanned product_done pair_added_pool states_summed
            y_taken gated_ready back_full taken_k0 taken_k1 pair_added_dve x1_ready wsel_loaded stored""".split()
        S = namedtuple("Signals", names)(*[sem(n) for n in names])
        x_loaded = (S.x_loaded0, S.x_loaded1)
        taken_k = (S.taken_k0, S.taken_k1)
        lora_loaded = (S.lora_loaded0, S.lora_loaded1)
        lora_merged = (S.lora_merged0, S.lora_merged1)
        lora_stored = (S.lora_stored0, S.lora_stored1)

        def c(name, k=0, p=slice(0, P)):
            return col[p, COLS[name] + k:COLS[name] + k + 1]

        def factors(e):
            room = wsel[0:2 * RANK, 2 * (e % 2):2 * (e % 2) + 2, :].rearrange("r a n -> r (a n)")
            return room[:, 0:HID], room[:, HID:HID + FF], room[:, HID + FF:HID + 2 * FF], room[:, HID + 2 * FF:2 * HID + 2 * FF]

        def staged(e):
            return hidA[:, 2 * (e % 2):2 * (e % 2) + 2, :].rearrange("p a n -> p (a n)")

        base = hidB[:, 0:2, :]

        x_g = x.rearrange("(g s b) (f j) h -> g (b f) s (j h)", s=2, b=2, j=2)
        out_g = out.rearrange("(g b) l h -> g l b h", b=GS)

        def front_at(g, fill):
            return g.number * FRONT_FILLS + (fill + 1)

        def back_at(g, fill):
            return g.number * BACK_FILLS + (fill + 1)

        def taken_at(g, fill):
            return g.number * BANK_FILLS[fill % 2] + (fill // 2 + 1 + 1)

        def unit_at(g, k):
            return g.number * UNITS + (k + 1)

        def pairs_before(k, pairs):
            return sum(1 for d in range(2) for q in pairs if 16 * d + 2 * q + 1 <= k)

        PAIRS = 2 * (len(POOL_PAIRS) + len(DVE_PAIRS))

        def token_order(t):
            return t.rearrange("p (n f j) -> p n f j", n=GS, j=2)

        def transposed_order(t):
            return t.rearrange("p (j n f) -> p n f j", j=2, n=GS)

        block = ctx.enter_context(nc.Block())

        @block.sync
        def _(sp):
            def load_x(g):
                if not (isinstance(g.turn, int) and g.turn == 0):
                    wait(sp, S.cond_done, g.number - 1)
                    wait(sp, S.resid_ready, g.number - 1)
                sp.dma_start(xin[:, g.parity].rearrange("p s j h -> p s (j h)"), x_g[g.number]).then_inc(x_loaded[g.parity], 16)

            def load_selected(g):
                chosen = [sp.value_load(expert_ids[0:1, bass.ds(g.number * GS + s, 1)], min_val=0, max_val=EXPERTS - 1)
                          for s in range(GS)]
                wait(sp, S.back_full, back_at(g, B_WO) - BACK_FILLS)
                for s in range(GS):
                    sp.dma_start(wsel[:, s, :], merged[bass.ds(chosen[s], 1)].rearrange("e p n -> p (e n)")).then_inc(S.wsel_loaded, 16)

            def store(g):
                sp.wait_ge(taken_k[B_TOK % 2], taken_at(g, B_TOK))
                sp.dma_start(out_g[g.number], tok[:, :].rearrange("l (b h) -> l b h", b=GS)).then_inc(S.stored, 16)

            g0, g1 = group(0, 0), group(0, 1)
            load_x(g0)
            for b in range(2):
                rows = slice(64 * b, 64 * b + 64)
                sp.dma_start(rot[rows, 0, :], delta_t[b:b + 1, :].to_broadcast([64, BATCH // 2])).then_inc(S.small_loaded, 16)
                sp.dma_start(freq_amp[rows, 0:1], frequencies).then_inc(S.small_loaded, 16)
                sp.dma_start(freq_amp[rows, 1:2], amplitudes).then_inc(S.small_loaded, 16)
            sp.dma_start(col[:, :], columns).then_inc(S.small_loaded, 16)
            sp.dma_start(w_in_s[:, :], w_in).then_inc(S.front_w_loaded, 16)
            sp.dma_start(w_x_s[:, :, :], w_x).then_inc(S.front_w_loaded, 16)
            sp.dma_start(w_dt_s[:, :], w_dt).then_inc(S.front_w_loaded, 16)
            load_x(g1)
            sp.dma_start(w_out_s, w_out).then_inc(S.fuse_w_loaded, 16)
            sp.dma_start(w_reduce_s, w_reduce).then_inc(S.fuse_w_loaded, 16)
            sp.dma_start(base[:, 0, :], wi).then_inc(S.base_loaded, 16)
            sp.dma_start(base[:, 1, :], wo).then_inc(S.base_loaded, 16)

            def store_merged(e):
                if e < EXPERTS - 1:
                    sp.wait_ge(lora_merged[e % 2], 2 * (e // 2 + 1))
                else:
                    sp.wait_ge(taken_k[0], 1)
                    sp.wait_ge(taken_k[1], 1)
                sp.dma_start(merged[e], staged(e)).then_inc(lora_stored[e % 2] if e < EXPERTS - 1 else S.stored, 16)

            for e in range(EXPERTS):
                if e >= 2:
                    sp.wait_ge(S.lora_full, 2 * (e - 1))
                wi_a, wi_b, wo_a, wo_b = factors(e)
                for dst, common, expert in ((wi_a, common_wi_a, experts_wi_a), (wi_b, common_wi_b, experts_wi_b),
                                            (wo_a, common_wo_a, experts_wo_a), (wo_b, common_wo_b, experts_wo_b)):
                    sp.dma_start(dst[0:RANK, :], common).then_inc(lora_loaded[e % 2], 16)
                    sp.dma_start(dst[RANK:2 * RANK, :], expert[e]).then_inc(lora_loaded[e % 2], 16)
                if e >= 1:
                    store_merged(e - 1)
            store_merged(EXPERTS - 1)
            for dst, src in ((w_glu_s[:, :], w_glu), (w1_s[:, :], w1), (w2_s[:, :], w2), (h1_s[:, :, :], h1),
                             (h2_s[:, :, :], h2), (w3_s[:, :, :], w3)):
                sp.dma_start(dst, src).then_inc(S.back_w_loaded, 16)
            sp.wait_ge(lora_stored[0], 16 * (EXPERTS // 2))
            sp.wait_ge(lora_stored[1], 16 * (EXPERTS // 2 - 1))
            sp.wait_ge(S.stored, 16)

            load_selected(g0)
            with sp.Fori(0, (NG - 2) // 2) as i:
                for k in (1, 2):
                    load_x(group(i, k + 1))
                    load_selected(group(i, k))
                    store(group(i, k - 1))
            last = group(0, NG - 1)
            load_selected(last)
            store(group(0, NG - 2))
            store(last)
            sp.wait_ge(S.stored, 16 * (NG + 1))

        @block.gpsimd
        def _(pool):
            nc.gpsimd.memset(ident[:, :], 0.0).then_inc(S.pick_zero, 1)
            pool.wait_ge(S.pick_zero, 1)
            nc.gpsimd.affine_select(out=ident[:, :], in_=ident[:, :], compare_op=ALU.not_equal, fill=1.0, base=0,
                                    pattern=[[-1, P]], channel_multiplier=1).then_inc(S.ident_ready, 1)
            nc.gpsimd.memset(pick[:, :], 0.0).then_inc(S.pick_step, 1)
            for part in range(3):
                pool.wait_ge(S.pick_step, part + 1)
                nc.gpsimd.affine_select(out=pick[:, :], in_=pick[:, :], compare_op=ALU.not_equal, fill=1.0,
                                        base=-32 * part, pattern=[[-1, 32]], channel_multiplier=1).then_inc(S.pick_step, 1)
            nc.gpsimd.memset(half_power[:, :], -0.5).then_inc(S.consts_ready, 1)

            def norm_power(g):
                wait(pool, S.consts_ready, 1)
                wait(pool, S.var_ready, g.number + 1)
                wait(pool, S.xn_ready, g.number)
                nc.gpsimd.tensor_tensor(rstd[:, :], var_eps[:, :], half_power[:, :], ALU.pow).then_inc(S.rstd_ready, 1)

            def residual(g):
                wait(pool, x_loaded[g.parity], g.turn * 16 + 16)
                wait(pool, S.cond_done, g.number + 1)
                wait(pool, S.back_full, back_at(g, B_RES) - 2 * BACK_FILLS)
                nc.gpsimd.tensor_tensor(resid[:, g.parity], xin[:, g.parity].rearrange("p s j h -> p j s h"),
                                        xc[:, :, :, :].rearrange("p s j h -> p j s h"), ALU.add).then_inc(S.resid_ready, 1)

            def step_sizes(g, d):
                wait(pool, S.log_ready, g.number * 2 + (d + 1))
                wait(pool, S.exp_done, unit_at(g, 16 * d + 15) - UNITS)
                nc.gpsimd.tensor_tensor(delta[:, d], relu_dt[:, :, :], log_dt[:, :, :], ALU.add).then_inc(S.delta_ready, 1)
                wait(pool, S.delta_ready, g.number * 2 + (d + 1))
                wait(pool, S.u_ready, g.number * 2 + 2)
                wait(pool, S.bx_ready, unit_at(g, 16 * d + 15) - UNITS)
                u = (u_f, u_r)[d]
                nc.gpsimd.tensor_tensor(du[:, d], delta[:, d], u[:, g.parity], ALU.mult).then_inc(S.du_ready, 1)

            def unit(g, k):
                d = k // NST
                if k % NST == 0:
                    pool.wait_ge(S.du_ready, g.number * 2 + (d + 1))
                pool.wait_ge(S.b_copied, unit_at(g, k))
                wait(pool, S.states_summed, unit_at(g, k) - RING)
                nc.gpsimd.tensor_tensor(state[:, k % RING], du[:, d],
                                        b_rows[:, k % 2, :].unsqueeze(1).to_broadcast([P, HALVES, GT]),
                                        ALU.mult).then_inc(S.bx_ready, 1)

            def add_pair(g, k):
                pool.wait_ge(S.product_done, unit_at(g, k))
                lo, hi = (k - 1) % RING, k % RING
                nc.gpsimd.tensor_tensor(state[:, lo], state[:, lo], state[:, hi], ALU.add).then_inc(S.pair_added_pool, 1)

            def period(i, c0, front, back):
                g, nxt = group(i, c0), group(i, c0 + 1)
                for k in range(UNITS):
                    unit(g, k)
                    p = k - 2
                    if p >= 0 and p % 2 == 1 and (p % 16) // 2 in POOL_PAIRS:
                        add_pair(g, p)
                    if k == DIR1_SLOT + 3:
                        step_sizes(g, 1)
                    if front and k == COND_SLOT + 1:
                        norm_power(nxt)
                    if front and k == COND_SLOT + 2:
                        residual(nxt)
                    if front and k == DIR0_SLOT + 4:
                        step_sizes(nxt, 0)
                if 15 // 2 in POOL_PAIRS or (31 % 16) // 2 in POOL_PAIRS:
                    add_pair(g, UNITS - 1)

            g0 = group(0, 0)
            norm_power(g0)
            residual(g0)
            step_sizes(g0, 0)
            period(0, 0, True, False)
            with pool.Fori(0, (NG - 2) // 2) as i:
                period(i, 1, True, True)
                period(i, 2, True, True)
            period(0, NG - 1, False, True)

        @block.scalar
        def _(act):
            def rotation_tables():
                act.wait_ge(S.small_loaded, 7 * 16)
                act.activation(rot[:, 2, 0:1], freq_amp[:, 1:2], ACT.Ln).then_inc(S.rot_act, 1)
                act.wait_ge(S.rot_act, 1)
                act.activation(rot[:, 3, :], rot[:, 0, :], ACT.Exp, scale=rot[:, 2, 0:1]).then_inc(S.rot_act, 1)
                act.activation(a_neg[:, :, :].rearrange("p h n -> p (h n)"), col[:, COLS["a_log"]:COLS["a_log"] + HALVES * NST],
                               ACT.Exp).then_inc(S.rot_act, 1)
                act.wait_ge(S.rot_dve, 4)
                act.activation(rot[:, 5, :], rot[:, 1, :], ACT.Abs).then_inc(S.rot_act, 1)
                act.wait_ge(S.rot_act, 4)
                act.activation(rot[:, 4, :], rot[:, 1, :], ACT.Sin).then_inc(S.rot_act, 1)
                act.wait_ge(S.consts_ready, 2)
                act.activation(rot[:, 6, :], rot[:, 5, :], ACT.Sin, scale=-1.0, bias=halfpi_col[:, 0:1]).then_inc(S.rot_act, 1)

            def scale_pairs(g):
                wait(act, x_loaded[g.parity], g.turn * 16 + 16)
                wait(act, S.rot_ready, 3)
                wait(act, S.cond_done, g.number)
                for s in range(2):
                    n = bass.ds(g.number * 2 + s, 1)
                    act.activation(scaled[:, s, 0], xin[:, g.parity, s, 0], ACT.Copy, scale=rot[:, 0, n])
                    ins = act.activation(scaled[:, s, 1], xin[:, g.parity, s, 0], ACT.Copy, scale=rot[:, 1, n])
                ins.then_inc(S.scaled_ready, 1)

            def norm_out(g):
                act.wait_ge(S.front_full, front_at(g, F_NORM))
                act.activation(token_order(xnT[:, :]), transposed_order(bank_f[:, :]), ACT.Identity,
                               scale=c("ln_g"), bias=c("ln_b")).then_inc(S.front_taken, 1)

            def conv_start(g, h):
                act.wait_ge(S.front_full, front_at(g, F_XI0 + h))
                wait(act, S.y_taken, g.number * 2 - 2)
                wait(act, S.u_ready, g.number * 2)
                wait(act, S.delta_ready, g.number * 2)
                tap = c("conv_w", h * TAPS + TAPS - 1)
                act.activation(u_f[:, g.parity, h], bank_f[:, :], ACT.Identity, scale=tap, bias=c("conv_b", h))
                act.activation(acc_r[:, h], bank_f[:, :], ACT.Identity, scale=tap, bias=c("conv_b", h)).then_inc(S.conv_init, 1)

            def silu_z(g, h):
                act.wait_ge(S.front_full, front_at(g, F_Z0 + h))
                wait(act, S.gated_ready, g.number * 2 - 2)
                act.activation(z[:, g.parity, h], bank_f[:, :], ACT.Silu).then_inc(S.front_taken, 1)

            def silu_u(g):
                act.wait_ge(S.front_taken, front_at(g, F_XI1))
                act.activation(u_f[:, g.parity], u_f[:, g.parity], ACT.Silu).then_inc(S.u_ready, 1)
                act.activation(u_r[:, g.parity, :, ::-1], acc_r[:, :, :], ACT.Silu).then_inc(S.u_ready, 1)

            def take_dbc(g, d):
                fill = (F_DBC0, F_DBC1)[d]
                act.wait_ge(S.front_full, front_at(g, fill))
                wait(act, S.c_full, unit_at(g, 16 * d + 15) - UNITS)
                act.activation(dtT[:, :], bank_f[0:DTR, :], ACT.Copy)
                act.activation(parts[0:32, d], bank_f[DTR:DTR + 32, :], ACT.Copy).then_inc(S.dt_copied, 1)

            def softplus_in(g, d, h):
                fill = (F_DT00, F_DT10)[d] + h
                act.wait_ge(S.front_full, front_at(g, fill))
                wait(act, S.delta_ready, g.number * 2 + d)
                act.wait_ge(S.u_ready, g.number * 2 + 2)
                act.activation(log_dt[:, h], bank_f[:, :], ACT.Abs, bias=c("dt_b", h)).then_inc(S.abs_ready, 1)
                act.activation(relu_dt[:, h], bank_f[:, :], ACT.Relu, bias=c("dt_b", h)).then_inc(S.front_taken, 1)

            def softplus_out(g, d):
                act.wait_ge(S.abs_ready, g.number * 4 + (2 * d + 2))
                act.activation(log_dt[:, :, :], log_dt[:, :, :], ACT.Exp, scale=-1.0).then_inc(S.exp_ready, 1)
                act.wait_ge(S.exp_ready, g.number * 2 + (d + 1))
                act.activation(log_dt[:, :, :], log_dt[:, :, :], ACT.Ln, bias=one_col[:, 0:1]).then_inc(S.log_ready, 1)

            def unit(g, k):
                d, n = k // NST, k % NST
                if n == 0:
                    act.wait_ge(S.delta_ready, g.number * 2 + (d + 1))
                act.wait_ge(S.b_full, unit_at(g, k))
                wait(act, S.bx_ready, unit_at(g, k) - 2)
                act.activation(b_rows[:, k % 2], bank_b[:, :], ACT.Copy).then_inc(S.b_copied, 1)
                wait(act, S.scanned, unit_at(g, k) - 2)
                for h in range(HALVES):
                    ins = act.activation(decay[:, k % 2, h, :, 1:], delta[:, d, h].rearrange("p (b t) -> p b t", b=GS)[:, :, 1:],
                                         ACT.Exp, scale=a_neg[:, h, n:n + 1])
                ins.then_inc(S.exp_done, 1)

            def take(g, fill, dst, func, **kw):
                act.wait_ge(S.back_full, back_at(g, fill))
                act.activation(dst, bank_k[fill % 2][:, :], func, **kw).then_inc(taken_k[fill % 2], 1)

            def back(g, k):
                if k == OUT_SLOT:
                    act.wait_ge(S.stored, g.number * 16 + 16)
                    take(g, B_OUT, gy[:, :], ACT.Gelu, bias=c("reduce_b"))
                if k == OUT_SLOT + 2:
                    wait(act, S.hb_ready, 1)
                    take(g, B_GLU0, glu_a[:, :], ACT.Identity, scale=0.5, bias=hb[:, 0:1])
                    take(g, B_GLU1, glu_t[:, :], ACT.Tanh, scale=0.5, bias=hb[:, 1:2])
                if k in HID_SLOTS:
                    for j in range(2):
                        f = 2 * HID_SLOTS.index(k) + j
                        take(g, B_HID + f, hidA[:, f], ACT.Relu)
                if k == WO_SLOT:
                    take(g, B_WO, cT[:, :], ACT.Copy)
                if k in GATE_SLOTS:
                    for j in range(2):
                        f = 2 * GATE_SLOTS.index(k) + j
                        if f >= 2:
                            act.wait_ge(taken_k[B_UP[f - 2] % 2], taken_at(g, B_UP[f - 2]))
                        take(g, B_GATE[f], gate[:, f % 2], ACT.Silu, scale=c("w1_s", f))
                if k in H1_SLOTS:
                    for j in range(2):
                        f = 2 * H1_SLOTS.index(k) + j
                        take(g, B_H1 + f, hidA[:, f], ACT.Gelu, scale=c("h1_s", f))
                if k in H2_SLOTS:
                    for j in range(2):
                        f = 2 * H2_SLOTS.index(k) + j
                        take(g, B_H2 + f, hidB[:, f], ACT.Gelu, scale=c("h2_s", f))
                if k == TOK_SLOT:
                    take(g, B_TOK, tok[:, :], ACT.Copy)

            def front(g, k):
                if k == COND_SLOT:
                    scale_pairs(g)
                if k == NORM_SLOT:
                    norm_out(g)
                if k == XI_SLOT:
                    conv_start(g, 0)
                if k == XI_SLOT + 1:
                    conv_start(g, 1)
                if k == Z_SLOTS[0]:
                    silu_z(g, 0)
                    silu_u(g)
                if k == Z_SLOTS[1]:
                    silu_z(g, 1)
                if k == DIR0_SLOT:
                    take_dbc(g, 0)
                if k == DIR0_SLOT + 2:
                    softplus_in(g, 0, 0)
                if k == DIR0_SLOT + 3:
                    softplus_in(g, 0, 1)
                    softplus_out(g, 0)

            def period(i, c0, with_front, with_back):
                g, nxt, prev = group(i, c0), group(i, c0 + 1), group(i, c0 - 1)
                for k in range(UNITS):
                    unit(g, k)
                    if k == DIR1_SLOT:
                        take_dbc(g, 1)
                    if k == DIR1_SLOT + 1:
                        softplus_in(g, 1, 0)
                    if k == DIR1_SLOT + 2:
                        softplus_in(g, 1, 1)
                        softplus_out(g, 1)
                    if with_front:
                        front(nxt, k)
                    if with_back:
                        back(prev, k)

            g0 = group(0, 0)
            rotation_tables()
            scale_pairs(g0)
            norm_out(g0)
            conv_start(g0, 0)
            conv_start(g0, 1)
            silu_z(g0, 0)
            silu_z(g0, 1)
            silu_u(g0)
            take_dbc(g0, 0)
            softplus_in(g0, 0, 0)
            softplus_in(g0, 0, 1)
            softplus_out(g0, 0)
            act.wait_ge(S.a_ready, 1)
            act.wait_ge(S.decay_zero, 1)
            period(0, 0, True, False)
            with act.Fori(0, (NG - 2) // 2) as i:
                period(i, 1, True, True)
                period(i, 2, True, True)
            period(0, NG - 1, False, True)
            for k in range(UNITS):
                back(group(0, NG - 1), k)

        @block.vector
        def _(dve):
            def rotation_tables():
                dve.memset(one_col[:, :], 1.0)
                dve.memset(halfpi_col[:, :], PI / 2).then_inc(S.consts_ready, 1)
                dve.memset(decay[:, :, :, :, :].rearrange("p a h b t -> p (a h b t)"), 0.0).then_inc(S.decay_zero, 1)
                dve.wait_ge(S.small_loaded, 7 * 16)
                dve.tensor_scalar(hb[:, :], col[:, COLS["glu_b"]:COLS["glu_b"] + 2], 0.5, None, ALU.mult).then_inc(S.hb_ready, 1)
                turn_hi = 6.28125
                turn_lo = 2 * PI - turn_hi
                big = 1.5 * 2.0 ** 23
                ang, turns, red = rot[:, 4, :], rot[:, 5, :], rot[:, 1, :]
                dve.tensor_scalar(ang, rot[:, 0, :], freq_amp[:, 0:1], None, ALU.mult).then_inc(S.rot_dve, 1)
                dve.wait_ge(S.rot_dve, 1)
                dve.tensor_scalar(turns, ang, 1.0 / (2 * PI), big, ALU.mult, ALU.add).then_inc(S.rot_ready, 1)
                dve.wait_ge(S.rot_ready, 1)
                dve.tensor_scalar(turns, turns, big, None, ALU.subtract).then_inc(S.rot_dve, 1)
                dve.wait_ge(S.rot_dve, 2)
                dve.scalar_tensor_tensor(rot[:, 7, :], turns, -turn_hi, ang, ALU.mult, ALU.add).then_inc(S.rot_dve, 1)
                dve.wait_ge(S.rot_dve, 3)
                dve.scalar_tensor_tensor(red, turns, -turn_lo, rot[:, 7, :], ALU.mult, ALU.add).then_inc(S.rot_ready, 1)
                dve.wait_ge(S.rot_ready, 2)
                dve.tensor_scalar(red, red, 3.1415925, -3.1415925, ALU.min, ALU.max).then_inc(S.rot_dve, 1)
                dve.wait_ge(S.rot_act, 6)
                dve.tensor_tensor(rot[:, 0, :], rot[:, 3, :], rot[:, 6, :], ALU.mult)
                dve.tensor_tensor(rot[:, 1, :], rot[:, 3, :], rot[:, 4, :], ALU.mult)
                dve.scalar_tensor_tensor(rot[:, 2, :], rot[:, 3, :], -1.0, rot[:, 4, :], ALU.mult, ALU.mult).then_inc(S.rot_ready, 1)
                dve.tensor_scalar(a_neg[:, :, :], a_neg[:, :, :], -1.0, None, ALU.mult).then_inc(S.a_ready, 1)
                dve.wait_ge(S.rot_ready, 3)

            def rotate(g):
                dve.wait_ge(S.scaled_ready, g.number + 1)
                wait(dve, S.resid_ready, g.number)
                wait(dve, S.xn_ready, g.number)
                for s in range(2):
                    n = bass.ds(g.number * 2 + s, 1)
                    x1 = xin[:, g.parity, s, 1]
                    dve.scalar_tensor_tensor(xc[:, s, 0], x1, rot[:, 2, n], scaled[:, s, 0], ALU.mult, ALU.add)
                    ins = dve.scalar_tensor_tensor(xc[:, s, 1], x1, rot[:, 0, n], scaled[:, s, 1], ALU.mult, ALU.add)
                ins.then_inc(S.cond_done, 1)
                dve.wait_ge(S.cond_done, g.number + 1)
                for t in range(GS):
                    ins = dve.bn_stats(stats[:, t], xc[:, t // 2, t % 2])
                ins.then_inc(S.stats_done, 1)
                dve.wait_ge(S.small_loaded, 7 * 16)
                dve.wait_ge(S.stats_done, g.number + 1)
                for t in range(GS):
                    ins = dve.bn_aggr(moments[:, t], stats[:, t])
                ins.then_inc(S.aggr_done, 1)
                dve.wait_ge(S.aggr_done, g.number + 1)
                wait(dve, S.rstd_ready, g.number)
                dve.tensor_scalar(var_eps[:, :], moments[:, :, 1], LN_EPS, None, ALU.add).then_inc(S.var_ready, 1)

            def normalise(g):
                dve.wait_ge(S.rstd_ready, g.number + 1)
                wait(dve, S.front_full, front_at(g, F_NORM) - FRONT_FILLS)
                for t in range(GS):
                    ins = dve.tensor_scalar(xn[:, t // 2, t % 2], xc[:, t // 2, t % 2], moments[:, t, 0:1], rstd[:, t:t + 1],
                                            ALU.subtract, ALU.mult)
                ins.then_inc(S.xn_ready, 1)

            def conv_taps(g, h):
                dve.wait_ge(S.conv_init, g.number * 2 + (h + 1))
                xi = bank_f[:, :].rearrange("p (b t) -> p b t", b=GS)
                fwd = u_f[:, g.parity, h].rearrange("p (b t) -> p b t", b=GS)
                rev = acc_r[:, h].rearrange("p (b t) -> p b t", b=GS)
                for m in range(1, TAPS):
                    tap = c("conv_w", h * TAPS + TAPS - 1 - m)
                    if m > 1:
                        dve.wait_ge(S.conv_tap, g.number * 8 + (4 * h + 2 * (m - 1) - 1))
                    ins = dve.scalar_tensor_tensor(fwd[:, :, m:], xi[:, :, :LEN - m], tap, fwd[:, :, m:], ALU.mult, ALU.add)
                    if m < TAPS - 1:
                        ins.then_inc(S.conv_tap, 1)
                        dve.wait_ge(S.conv_tap, g.number * 8 + (4 * h + 2 * (m - 1))) if m > 1 else None
                    else:
                        dve.wait_ge(S.conv_tap, g.number * 8 + (4 * h + 4))
                    ins = dve.scalar_tensor_tensor(rev[:, :, :LEN - m], xi[:, :, m:], tap, rev[:, :, :LEN - m], ALU.mult, ALU.add)
                    ins.then_inc(S.conv_tap if m < TAPS - 1 else S.front_taken, 1)

            def split_rows(g, d):
                dve.wait_ge(S.dt_copied, g.number * 2 + (d + 1))
                dve.tensor_tensor(rest[32:64, :], bank_f[DTR:DTR + 32, :], parts[0:32, d], ALU.subtract).then_inc(S.front_taken, 1)
                dve.wait_ge(S.front_taken, front_at(g, (F_DBC0, F_DBC1)[d]))
                dve.tensor_copy(parts[32:64, d], rest[32:64, :]).then_inc(S.mid_ready, 1)
                dve.wait_ge(S.mid_ready, g.number * 2 + (d + 1))
                dve.tensor_tensor(parts[64:96, d], rest[32:64, :], parts[32:64, d], ALU.subtract).then_inc(S.parts_ready, 1)

            def unit(g, k):
                dve.wait_ge(S.exp_done, unit_at(g, k))
                dve.wait_ge(S.bx_ready, unit_at(g, k))
                st = state[:, k % RING].rearrange("p h t -> p (h t)")
                dve.tensor_tensor_scan(st, decay[:, k % 2].rearrange("p h b t -> p (h b t)"), st, 0.0,
                                       ALU.mult, ALU.add).then_inc(S.scanned, 1)

            def weigh(g, k):
                dve.wait_ge(S.scanned, unit_at(g, k))
                dve.wait_ge(S.c_full, unit_at(g, k))
                dve.tensor_tensor(state[:, k % RING], state[:, k % RING],
                                  bank_c[k % 2][:, :].unsqueeze(1).to_broadcast([P, HALVES, GT]), ALU.mult).then_inc(S.product_done, 1)

            def add_pair(g, k):
                dve.wait_ge(S.product_done, unit_at(g, k))
                lo, hi = (k - 1) % RING, k % RING
                dve.tensor_tensor(state[:, lo], state[:, lo], state[:, hi], ALU.add).then_inc(S.pair_added_dve, 1)

            def take_y(g, d):
                dve.wait_ge(S.states_summed, unit_at(g, 16 * d + 15))
                wait(dve, S.gated_ready, g.number * 2 + d)
                u = (u_f, u_r)[d]
                for h in range(HALVES):
                    dst = ysum[:, h, :] if d == 0 else ysum[:, h, ::-1]
                    ins = dve.scalar_tensor_tensor(dst, u[:, g.parity, h], c("skip_d", h), bank_y[:, h], ALU.mult, ALU.add)
                ins.then_inc(S.y_taken, 1)
                dve.wait_ge(S.y_taken, g.number * 2 + (d + 1))
                wait(dve, S.back_full, back_at(g, B_OUT) - BACK_FILLS)
                dve.tensor_tensor(gated[:, d], ysum[:, :, :], z[:, g.parity], ALU.mult).then_inc(S.gated_ready, 1)

            def back(g, k):
                if k == OUT_SLOT + 3:
                    dve.wait_ge(taken_k[0], taken_at(g, B_GLU1))
                    dve.wait_ge(taken_k[1], taken_at(g, B_GLU0))
                    dve.scalar_tensor_tensor(x1T[:, :], glu_t[:, :], 1.0, glu_a[:, :], ALU.add, ALU.mult).then_inc(S.x1_ready, 1)
                    dve.wait_ge(S.x1_ready, g.number + 1)
                    dve.wait_ge(S.back_full, back_at(g, B_RES))
                    dve.tensor_tensor(token_order(x1T[:, :]), token_order(x1T[:, :]), transposed_order(bank_k[B_RES % 2][:, :]),
                                      ALU.add).then_inc(taken_k[B_RES % 2], 1)
                if k in UP_SLOTS:
                    for j in range(2):
                        f = 2 * UP_SLOTS.index(k) + j
                        dve.wait_ge(S.back_full, back_at(g, B_UP[f]))
                        dve.wait_ge(taken_k[B_GATE[f] % 2], taken_at(g, B_GATE[f]))
                        dve.scalar_tensor_tensor(hidB[:, f], bank_k[B_UP[f] % 2][:, :], c("w2_s", f), gate[:, f % 2],
                                                 ALU.mult, ALU.mult).then_inc(taken_k[B_UP[f] % 2], 1)
                if k == W3_SLOT:
                    dve.wait_ge(S.back_full, back_at(g, B_W3))
                    dve.scalar_tensor_tensor(oT[:, :], bank_k[B_W3 % 2][:, :], c("w3_s"), x1T[:, :],
                                             ALU.mult, ALU.add).then_inc(taken_k[B_W3 % 2], 1)

            def merge(e):
                if e == 0:
                    dve.wait_ge(S.base_loaded, 32)
                    dve.wait_ge(S.fused_full, 1)
                    dve.tensor_copy(w_fused[:, :, :, :].rearrange("p d h o -> p (d h o)"), bank_k[0][:, :]).then_inc(S.fused_ready, 1)
                for part in range(2):
                    dve.wait_ge(S.lora_full, 2 * e + part + 1)
                    if e >= 2:
                        dve.wait_ge(lora_stored[e % 2], 16 * (e // 2))
                    dve.scalar_tensor_tensor(staged(e)[:, part * FF:(part + 1) * FF], bank_k[part][:, :], LORA_ALPHA, base[:, part],
                                             ALU.mult, ALU.add).then_inc(lora_merged[e % 2] if e < EXPERTS - 1 else taken_k[part], 1)

            def front(g, k):
                if k == COND_SLOT:
                    rotate(g)
                if k == COND_SLOT + 2:
                    normalise(g)
                if k == XI_SLOT:
                    conv_taps(g, 0)
                if k == XI_SLOT + 1:
                    conv_taps(g, 1)
                if k == DIR0_SLOT:
                    split_rows(g, 0)

            def period(i, c0, with_front, with_back):
                g, nxt, prev = group(i, c0), group(i, c0 + 1), group(i, c0 - 1)
                for k in range(UNITS):
                    unit(g, k)
                    if k > 0:
                        weigh(g, k - 1)
                    p = k - 2
                    if p >= 0 and p % 2 == 1 and (p % 16) // 2 in DVE_PAIRS:
                        add_pair(g, p)
                    if k == DIR1_SLOT:
                        split_rows(g, 1)
                    if k == NST + 3:
                        take_y(g, 0)
                    if with_front:
                        front(nxt, k)
                    if with_back:
                        back(prev, k)
                    elif k in MERGE_SLOTS:
                        merge(MERGE_SLOTS.index(k))
                weigh(g, UNITS - 1)
                if (31 % 16) // 2 in DVE_PAIRS:
                    add_pair(g, UNITS - 1)
                take_y(g, 1)

            g0 = group(0, 0)
            rotation_tables()
            rotate(g0)
            dve.wait_ge(S.pick_step, 4)
            dve.tensor_copy(spread[:, :, :], pick[:, :].unsqueeze(2).to_broadcast([96, 32, P])).then_inc(S.spread_ready, 1)
            normalise(g0)
            conv_taps(g0, 0)
            conv_taps(g0, 1)
            split_rows(g0, 0)
            period(0, 0, True, False)
            with dve.Fori(0, (NG - 2) // 2) as i:
                period(i, 1, True, True)
                period(i, 2, True, True)
            period(0, NG - 1, False, True)
            for k in range(UNITS):
                back(group(0, NG - 1), k)

        @block.tensor
        def _(pe):
            def fill_front(g, fill):
                wait(pe, S.front_taken, front_at(g, fill) - 1)

            def transpose_norm(g):
                wait(pe, S.ident_ready, 1)
                pe.wait_ge(S.xn_ready, g.number + 1)
                fill_front(g, F_NORM)
                for t in range(GS):
                    s, j = t // 2, t % 2
                    at = (2 * j + s) * P
                    ins = pe.transpose(bank_f[:, at:at + P], xn[:, s, j], ident[:, :])
                ins.then_inc(S.front_full, 1)

            def project_in(g, fill):
                m = fill - F_XI0
                wait(pe, S.front_w_loaded, 48)
                fill_front(g, fill)
                pe.matmul(bank_f[:, :], w_in_s[:, m * P:(m + 1) * P], xnT[:, :], start=True, stop=True).then_inc(S.front_full, 1)

            def project_x(g, d):
                fill = (F_DBC0, F_DBC1)[d]
                fill_front(g, fill)
                pe.wait_ge(S.u_ready, g.number * 2 + 2)
                u = (u_f, u_r)[d]
                for h in range(HALVES):
                    ins = pe.matmul(bank_f[0:DTR + 2 * NST, :], w_x_s[:, h], u[:, g.parity, h], start=(h == 0), stop=(h == HALVES - 1))
                ins.then_inc(S.front_full, 1)

            def project_dt(g, d, h):
                fill = (F_DT00, F_DT10)[d] + h
                fill_front(g, fill)
                pe.wait_ge(S.dt_copied, g.number * 2 + (d + 1))
                pe.matmul(bank_f[:, :], w_dt_s[:, h * P:(h + 1) * P], dtT[:, :], start=True, stop=True).then_inc(S.front_full, 1)

            def spread_b(g, k):
                d, n = k // NST, k % NST
                if n == 0:
                    pe.wait_ge(S.parts_ready, g.number * 2 + (d + 1))
                wait(pe, S.b_copied, unit_at(g, k) - 1)
                pe.matmul(bank_b[:, :], spread[:, n], parts[:, d], start=True, stop=True).then_inc(S.b_full, 1)

            def spread_c(g, k):
                d, n = k // NST, k % NST
                wait(pe, S.product_done, unit_at(g, k) - 2)
                pe.matmul(bank_c[k % 2][:, :], spread[:, NST + n], parts[:, d], start=True, stop=True).then_inc(S.c_full, 1)

            def sum_states(g, k):
                d, n = k // NST, k % NST
                q = n // 2
                if q in POOL_PAIRS:
                    pe.wait_ge(S.pair_added_pool, g.number * (2 * len(POOL_PAIRS)) + pairs_before(k, POOL_PAIRS))
                    sources = (k - 1,)
                elif q in DVE_PAIRS:
                    pe.wait_ge(S.pair_added_dve, g.number * (2 * len(DVE_PAIRS)) + pairs_before(k, DVE_PAIRS))
                    sources = (k - 1,)
                else:
                    pe.wait_ge(S.product_done, unit_at(g, k))
                    sources = (k - 1, k)
                if n == 1:
                    wait(pe, S.y_taken, g.number * 2 + d)
                for src in sources:
                    for h in range(HALVES):
                        ins = pe.matmul(bank_y[:, h], ident[:, :], state[:, src % RING, h], start=(n == 1 and src == sources[0]),
                                        stop=(n == NST - 1 and src == sources[-1]))
                ins.then_inc(S.states_summed, 2)

            def fill_back(g, fill, *sources):
                for bank in range(2):
                    fills = [f for f in (fill - 2, *sources) if f % 2 == bank]
                    if fills:
                        wait(pe, taken_k[bank], taken_at(g, max(fills)))

            def back(g, k):
                if k == OUT_SLOT:
                    wait(pe, S.fused_ready, 1)
                    pe.wait_ge(S.gated_ready, g.number * 2 + 2)
                    fill_back(g, B_OUT)
                    for d in range(2):
                        for h in range(HALVES):
                            ins = pe.matmul(bank_k[0][:, :], w_fused[:, d, h], gated[:, d, h], start=(d == 0 and h == 0),
                                            stop=(d == 1 and h == HALVES - 1))
                    ins.then_inc(S.back_full, 1)
                if k == OUT_SLOT + 2:
                    wait(pe, S.back_w_loaded, 6 * 16)
                    for m in range(2):
                        fill_back(g, B_GLU0 + m, B_OUT)
                        pe.matmul(bank_k[(B_GLU0 + m) % 2][:, :], w_glu_s[:, m * P:(m + 1) * P], gy[:, :], start=True,
                                  stop=True).then_inc(S.back_full, 1)
                if k == OUT_SLOT + 3:
                    fill_back(g, B_RES)
                    pe.wait_ge(S.resid_ready, g.number + 1)
                    for t in range(GS):
                        ins = pe.transpose(bank_k[B_RES % 2][:, t * P:(t + 1) * P], resid[:, g.parity, t // 2, t % 2], ident[:, :])
                    ins.then_inc(S.back_full, 1)
                if k in HID_SLOTS:
                    pe.wait_ge(S.wsel_loaded, g.number * (16 * GS) + 16 * GS)
                    for j in range(2):
                        f = 2 * HID_SLOTS.index(k) + j
                        fill_back(g, B_HID + f, B_RES)
                        for s in range(GS):
                            ins = pe.matmul(bank_k[f % 2][:, s * LEN:(s + 1) * LEN], wsel[:, s, f * P:(f + 1) * P],
                                            x1T[:, s * LEN:(s + 1) * LEN], start=True, stop=True)
                        ins.then_inc(S.back_full, 1)
                if k == WO_SLOT:
                    fill_back(g, B_WO, *range(B_HID, B_HID + FC))
                    for s in range(GS):
                        for f in range(FC):
                            ins = pe.matmul(bank_k[B_WO % 2][:, s * LEN:(s + 1) * LEN], wsel[:, s, FF + f * HID:FF + (f + 1) * HID],
                                            hidA[:, f, s * LEN:(s + 1) * LEN], start=(f == 0), stop=(f == FC - 1))
                    ins.then_inc(S.back_full, 1)
                for slots, fills, w in ((GATE_SLOTS, B_GATE, w1_s), (UP_SLOTS, B_UP, w2_s)):
                    if k in slots:
                        for j in range(2):
                            f = 2 * slots.index(k) + j
                            fill_back(g, fills[f], B_WO)
                            pe.matmul(bank_k[fills[f] % 2][:, :], w[:, f * P:(f + 1) * P], cT[:, :], start=True,
                                      stop=True).then_inc(S.back_full, 1)
                for slots, first, w, src, before in ((H1_SLOTS, B_H1, h1_s, hidB, B_UP), (H2_SLOTS, B_H2, h2_s, hidA, range(B_H1, B_H1 + FC))):
                    if k in slots:
                        for j in range(2):
                            f = 2 * slots.index(k) + j
                            fill_back(g, first + f, *before)
                            for q in range(FC):
                                ins = pe.matmul(bank_k[(first + f) % 2][:, :], w[:, q, f * P:(f + 1) * P], src[:, q],
                                                start=(q == 0), stop=(q == FC - 1))
                            ins.then_inc(S.back_full, 1)
                if k == W3_SLOT:
                    fill_back(g, B_W3, *range(B_H2, B_H2 + FC))
                    for q in range(FC):
                        ins = pe.matmul(bank_k[B_W3 % 2][:, :], w3_s[:, q], hidB[:, q], start=(q == 0), stop=(q == FC - 1))
                    ins.then_inc(S.back_full, 1)
                if k == TOK_SLOT:
                    fill_back(g, B_TOK, B_W3)
                    for s in range(GS):
                        ins = pe.transpose(bank_k[B_TOK % 2][:, s * P:(s + 1) * P], oT[:, s * LEN:(s + 1) * LEN], ident[:, :])
                    ins.then_inc(S.back_full, 1)

            def fuse_out():
                pe.wait_ge(S.fuse_w_loaded, 32)
                for d in range(2):
                    for h in range(HALVES):
                        at = (d * HALVES + h) * HID
                        ins = pe.matmul(bank_k[0][:, at:at + HID], w_out_s[:, h * P:(h + 1) * P], w_reduce_s[:, d], start=True, stop=True)
                ins.then_inc(S.fused_full, 1)

            def merge(e):
                wi_a, wi_b, wo_a, wo_b = factors(e)
                pe.wait_ge(lora_loaded[e % 2], 16 * 8 * (e // 2 + 1))
                if e == 0:
                    pe.wait_ge(S.fused_ready, 1)
                else:
                    pe.wait_ge(lora_merged[(e - 1) % 2], 2 * ((e - 1) // 2 + 1))
                pe.matmul(bank_k[0][:, :], wi_a, wi_b, start=True, stop=True).then_inc(S.lora_full, 1)
                for f in range(FC):
                    ins = pe.matmul(bank_k[1][:, f * HID:(f + 1) * HID], wo_a[:, f * P:(f + 1) * P], wo_b, start=True, stop=True)
                ins.then_inc(S.lora_full, 1)

            def front(g, k):
                if k == NORM_SLOT:
                    transpose_norm(g)
                if k == XI_SLOT:
                    project_in(g, F_XI0)
                if k == XI_SLOT + 1:
                    project_in(g, F_XI1)
                if k == Z_SLOTS[0]:
                    project_in(g, F_Z0)
                if k == Z_SLOTS[1]:
                    project_in(g, F_Z1)
                if k == DIR0_SLOT:
                    project_x(g, 0)
                if k == DIR0_SLOT + 2:
                    project_dt(g, 0, 0)
                if k == DIR0_SLOT + 3:
                    project_dt(g, 0, 1)

            def period(i, c0, with_front, with_back):
                g, nxt, prev = group(i, c0), group(i, c0 + 1), group(i, c0 - 1)
                spread_b(g, 0)
                spread_c(g, 0)
                for k in range(UNITS):
                    if k == DIR1_SLOT:
                        project_x(g, 1)
                    if k == DIR1_SLOT + 1:
                        project_dt(g, 1, 0)
                    if k == DIR1_SLOT + 2:
                        project_dt(g, 1, 1)
                    if k + 1 < UNITS:
                        spread_b(g, k + 1)
                        spread_c(g, k + 1)
                    p = k - 3
                    if p >= 0 and p % 2 == 1:
                        sum_states(g, p)
                    if with_front:
                        front(nxt, k)
                    if with_back:
                        back(prev, k)
                    elif k in MERGE_SLOTS:
                        if k == MERGE_SLOTS[0]:
                            fuse_out()
                        merge(MERGE_SLOTS.index(k))
                sum_states(g, UNITS - 3)
                sum_states(g, UNITS - 1)

            g0 = group(0, 0)
            transpose_norm(g0)
            for fill in (F_XI0, F_XI1, F_Z0, F_Z1):
                project_in(g0, fill)
            project_x(g0, 0)
            project_dt(g0, 0, 0)
            project_dt(g0, 0, 1)
            pe.wait_ge(S.spread_ready, 1)
            period(0, 0, True, False)
            with pe.Fori(0, (NG - 2) // 2) as i:
                period(i, 1, True, True)
                period(i, 2, True, True)
            period(0, NG - 1, False, True)
            for k in range(UNITS):
                back(group(0, NG - 1), k)


DIR1_SLOT = 1
COND_SLOT = 3
NORM_SLOT = 7
XI_SLOT = 8
Z_SLOTS = (12, 14)
DIR0_SLOT = 18
OUT_SLOT = 0
HID_SLOTS = (5, 6)
WO_SLOT = 8
GATE_SLOTS = (12, 14)
UP_SLOTS = (13, 15)
H1_SLOTS = (17, 19)
H2_SLOTS = (22, 24)
W3_SLOT = 27
TOK_SLOT = 29
MERGE_SLOTS = tuple(range(6, 6 + 2 * EXPERTS, 2))


def kernel(**inputs):
    import concourse.bacc as _bacc
    from concourse.bass_utils import run_bass_kernel_spmd as _run

    def host(name):
        return np.asarray(inputs[name])

    def halves(a):
        return a.reshape(HALVES, P, -1).transpose(1, 0, 2).reshape(P, -1)

    def chunked(a):
        return a.reshape(-1, P, a.shape[1]).transpose(1, 0, 2)

    attn, cond2, ffn = "L0_attn_", "L0_cond2_", "L0_ffn_"
    columns = np.concatenate([
        halves(host(attn + "conv_w").reshape(DI, TAPS)), halves(host(attn + "conv_b")), halves(host(attn + "dt_proj_b")),
        halves(host(attn + "D")), halves(host(attn + "A_log")), host(attn + "ln_g").reshape(P, 1), host(attn + "ln_b").reshape(P, 1),
        host(attn + "dim_reduce_b").reshape(P, 1), halves(host(attn + "glu_b")),
        host(ffn + "w1_s").reshape(FC, P).T, host(ffn + "w2_s").reshape(FC, P).T, host(ffn + "h1_s").reshape(FC, P).T,
        host(ffn + "h2_s").reshape(FC, P).T, host(ffn + "w3_s").reshape(P, 1)], axis=1)
    arrays = {
        "x": host("x"), "delta_t": host("condB_deltat").reshape(BATCH // 2, 2).T, "expert_ids": host("itok_B_0_7").reshape(1, BATCH),
        "amplitudes": host("L0_cond_amplitudes").reshape(-1, 1), "frequencies": host("L0_cond_frequencies").reshape(-1, 1),
        "columns": columns,
        "w_in": host(attn + "in_proj_w").T, "w_x": chunked(host(attn + "x_proj_w").T), "w_dt": host(attn + "dt_proj_w").T,
        "w_out": host(attn + "out_proj_w"), "w_reduce": chunked(host(attn + "dim_reduce_w").T), "w_glu": host(attn + "glu_w").T,
        "wi": host(cond2 + "wi").T, "wo": chunked(host(cond2 + "wo").T).reshape(P, FF),
        "common_wi_a": host(cond2 + "common_wi_a"), "common_wi_b": host(cond2 + "common_wi_b").T,
        "common_wo_a": host(cond2 + "common_wo_a"), "common_wo_b": host(cond2 + "common_wo_b").T,
        "experts_wi_a": host(cond2 + "experts_wi_a"), "experts_wi_b": host(cond2 + "experts_wi_b").transpose(0, 2, 1),
        "experts_wo_a": host(cond2 + "experts_wo_a"), "experts_wo_b": host(cond2 + "experts_wo_b").transpose(0, 2, 1),
        "w1": host(ffn + "w1_w").T, "w2": host(ffn + "w2_w").T, "h1": chunked(host(ffn + "h1_w").T),
        "h2": chunked(host(ffn + "h2_w").T), "w3": chunked(host(ffn + "w3_w").T),
    }
    arrays = {f"in_{k}": np.ascontiguousarray(v) for k, v in arrays.items()}
    nc = _bacc.Bacc("TRN2", target_bir_lowering=False, num_devices=1)
    args = [nc.dram_tensor(k, v.shape, mybir.dt.from_np(v.dtype), kind="ExternalInput").ap() for k, v in arrays.items()]
    args.append(nc.dram_tensor("merged", (EXPERTS, P, 2 * FF), F32, kind="Internal").ap())
    args.append(nc.dram_tensor("out", (BATCH, LEN, HID), F32, kind="ExternalOutput").ap())
    build(nc, *args)
    r = _run(nc, [arrays], core_ids=[0])
    return r.results[0]["out"]
```

```python
from collections import namedtuple
from contextlib import ExitStack

import numpy as np

import concourse.bass as bass
from concourse import mybir

F32 = mybir.dt.float32
BF16 = mybir.dt.bfloat16
I32 = mybir.dt.int32
ALU = mybir.AluOpType
ACT = mybir.ActivationFunctionType

P = 128
BATCH, LEN, HID = 32, 128, 128
DI, NST, TAPS, DTR = 256, 16, 4, 64
EXPERTS, RANK, FF = 8, 16, 512
LN_EPS, LORA_ALPHA = 1e-5, 2.0

GS = 4
NG = BATCH // GS
GT = GS * LEN
HALVES = DI // P
FC = FF // P
UNITS = 2 * NST
RING = 8
DECAYS = 4

COLS = {}
_at = 0
for _name, _n in (("conv_w", HALVES * TAPS), ("conv_b", HALVES), ("dt_b", HALVES), ("skip_d", HALVES),
                  ("a_log", HALVES * NST), ("ln_g", 1), ("ln_b", 1), ("reduce_b", 1), ("glu_b", 2),
                  ("w1_s", FC), ("w2_s", FC), ("h1_s", FC), ("h2_s", FC), ("w3_s", 1)):
    COLS[_name] = _at
    _at += _n
NCOLS = _at

(F_NORM, F_XI0, F_XI1, F_Z0, F_Z1, F_DBC0, F_DT00, F_DT01, F_DBC1, F_DT10, F_DT11) = range(11)
FRONT_FILLS = 11
B_OUT, B_GLU0, B_GLU1, B_RES = range(4)
B_HID, B_WO = range(4, 8), 8
B_GATE = (9, 10, 13, 14)
B_UP = (11, 12, 15, 16)
B_H1, B_H2, B_W3, B_TOK = range(17, 21), range(21, 25), 25, 26
BACK_FILLS = 27
BANK_FILLS = ((BACK_FILLS + 1) // 2, BACK_FILLS // 2)

Group = namedtuple("Group", "number parity turn")


def group(i, c):
    return Group(i * 2 + c, c % 2, i + c // 2)


def wait(eng, signal, value):
    if isinstance(value, int) and value <= 0:
        return
    eng.wait_ge(signal, value)


def build(nc, x, delta_t, expert_ids, amplitudes, frequencies, columns, w_in, w_x, w_dt, w_out, w_reduce, w_glu,
          wi, wo, common_wi_a, common_wi_b, common_wo_a, common_wo_b,
          experts_wi_a, experts_wi_b, experts_wo_a, experts_wo_b, w1, w2, h1, h2, w3, merged, out):
    PI = float(np.pi)
    ctx = ExitStack()
    with ctx:
        def sb(name, shape, dt=F32):
            return ctx.enter_context(nc.sbuf_tensor(name, shape, dt))

        def sem(name):
            return ctx.enter_context(nc.semaphore(name))

        col = sb("col", [P, NCOLS])
        w_in_s = sb("w_in_s", [P, 2 * DI])
        w_x_s = sb("w_x_s", [P, HALVES, DTR + 2 * NST])
        w_dt_s = sb("w_dt_s", [DTR, DI])
        w_fused = sb("w_fused", [P, 2, HALVES, HID])
        w_glu_s = sb("w_glu_s", [P, 2 * HID])
        w1_s = sb("w1_s", [P, FF])
        w2_s = sb("w2_s", [P, FF])
        h1_s = sb("h1_s", [P, FC, FF])
        h2_s = sb("h2_s", [P, FC, FF])
        w3_s = sb("w3_s", [P, FC, HID])
        ident = sb("ident", [P, P])
        pick = sb("pick", [96, 32], BF16)
        a_neg = sb("a_neg", [P, HALVES, NST])
        hb = sb("hb", [P, 2])
        rot = sb("rot", [P, 8, BATCH // 2])
        half_power = sb("half_power", [P, GS])
        one_col = sb("one_col", [P, 1])
        halfpi_col = sb("halfpi_col", [P, 1])
        freq_amp = sb("freq_amp", [P, 2])

        xin = sb("xin", [P, 2, 2, 2, HID])
        scaled = sb("scaled", [P, 2, 2, HID])
        xc = sb("xc", [P, 2, 2, HID])
        xn = scaled
        stats = sb("stats", [P, GS, 6])
        moments = sb("moments", [P, GS, 2])
        var_eps = sb("var_eps", [P, GS])
        rstd = sb("rstd", [P, GS])
        resid = sb("resid", [P, 2, 2, 2, HID])
        xnT = sb("xnT", [P, GT])
        u_f = sb("u_f", [P, 2, HALVES, GT])
        u_r = sb("u_r", [P, 2, HALVES, GT])
        z = sb("z", [P, 2, HALVES, GT])
        dtT = sb("dtT", [DTR, GT])
        parts = sb("parts", [96, 2, GT], BF16)
        rest = sb("rest", [64, GT])
        relu_dt = sb("relu_dt", [P, HALVES, GT])
        acc_r = relu_dt
        log_dt = sb("log_dt", [P, HALVES, GT])
        delta = sb("delta", [P, 2, HALVES, GT])
        du = sb("du", [P, 2, HALVES, GT])

        decay = sb("decay", [P, DECAYS, HALVES, GS, LEN])
        b_rows = sb("b_rows", [P, 2, GT])
        state = sb("state", [P, RING, HALVES, GT])

        ysum = sb("ysum", [P, HALVES, GT])
        y_rows = ysum
        gated = sb("gated", [P, 2, HALVES, GT])
        gy = sb("gy", [P, GT])
        glu_a = sb("glu_a", [P, GT])
        glu_t = sb("glu_t", [P, GT])
        x1T = sb("x1T", [P, GT])
        wsel = sb("wsel", [P, GS, 2 * FF])
        hidA = sb("hidA", [P, FC, GT])
        hidB = sb("hidB", [P, FC, GT])
        cT = glu_a
        gate = sb("gate", [P, 2, GT])
        tok = gate[:, 0, :]
        w_out_s = gate[:, 0, 0:DI]
        w_reduce_s = gate[:, 1, 0:2 * HID].rearrange("p (d o) -> p d o", d=2)
        oT = glu_t

        bank_b = ctx.enter_context(nc.psum_tensor("bank_b", [P, GT], F32))
        bank_c = [ctx.enter_context(nc.psum_tensor(f"bank_c{i}", [P, GT], F32)) for i in range(2)]
        bank_y = ctx.enter_context(nc.psum_tensor("bank_y", [P, HALVES, GT], F32))
        bank_f = ctx.enter_context(nc.psum_tensor("bank_f", [P, GT], F32))
        bank_k = [ctx.enter_context(nc.psum_tensor(f"bank_k{i}", [P, GT], F32)) for i in range(2)]

        names = """small_loaded front_w_loaded fuse_w_loaded back_w_loaded lora_loaded0 lora_loaded1 base_loaded
            ident_ready pick_zero pick_step consts_ready decay_zero rot_act rot_dve rot_ready a_ready
            hb_ready fused_full fused_ready lora_full lora_merged0 lora_merged1 lora_stored0 lora_stored1
            x_loaded0 x_loaded1 scaled_ready cond_done stats_done aggr_done var_ready rstd_ready xn_ready resid_ready
            front_full front_taken conv_init conv_tap u_ready dt_copied rest_ready mid_ready parts_ready
            relu_ready abs_ready exp_ready log_ready delta_ready du_ready
            b_full b_copied c_full exp_done bx_ready scanned product_done states_summed
            y_taken gated_ready back_full taken_k0 taken_k1 y_copied y_turned x1_ready wsel_loaded stored""".split()
        S = namedtuple("Signals", names)(*[sem(n) for n in names])
        x_loaded = (S.x_loaded0, S.x_loaded1)
        taken_k = (S.taken_k0, S.taken_k1)
        lora_loaded = (S.lora_loaded0, S.lora_loaded1)
        lora_merged = (S.lora_merged0, S.lora_merged1)
        lora_stored = (S.lora_stored0, S.lora_stored1)

        def c(name, k=0, p=slice(0, P)):
            return col[p, COLS[name] + k:COLS[name] + k + 1]

        def factors(e):
            room = wsel[0:2 * RANK, 2 * (e % 2):2 * (e % 2) + 2, :].rearrange("r a n -> r (a n)")
            return room[:, 0:HID], room[:, HID:HID + FF], room[:, HID + FF:HID + 2 * FF], room[:, HID + 2 * FF:2 * HID + 2 * FF]

        def staged(e):
            return hidA[:, 2 * (e % 2):2 * (e % 2) + 2, :].rearrange("p a n -> p (a n)")

        base = hidB[:, 0:2, :]

        x_g = x.rearrange("(g s b) (f j) h -> g (b f) s (j h)", s=2, b=2, j=2)
        out_g = out.rearrange("(g b) l h -> g l b h", b=GS)

        def front_at(g, fill):
            return g.number * FRONT_FILLS + (fill + 1)

        def back_at(g, fill):
            return g.number * BACK_FILLS + (fill + 1)

        def taken_at(g, fill):
            return g.number * BANK_FILLS[fill % 2] + (fill // 2 + 1 + 1)

        def unit_at(g, k):
            return g.number * UNITS + (k + 1)

        def around(groups, k):
            j, unit = divmod(k, UNITS)
            return (groups[j], unit) if j in groups else (None, unit)

        def run(eng, period):
            def at(i, c, present):
                period({j: group(i, c + j) for j in present})

            at(0, -1, (1,))
            at(0, 0, (0, 1))
            at(0, 1, (-1, 0, 1))
            with eng.Fori(0, (NG - 4) // 2) as i:
                at(i, 2, (-2, -1, 0, 1))
                at(i, 3, (-2, -1, 0, 1))
            at(0, NG - 2, (-2, -1, 0, 1))
            at(0, NG - 1, (-2, -1, 0))
            at(0, NG, (-2, -1))
            at(0, NG + 1, (-2,))

        def token_order(t):
            return t.rearrange("p (n f j) -> p n f j", n=GS, j=2)

        def transposed_order(t):
            return t.rearrange("p (j n f) -> p n f j", j=2, n=GS)

        block = ctx.enter_context(nc.Block())

        @block.sync
        def _(sp):
            def load_x(g):
                if not (isinstance(g.turn, int) and g.turn == 0):
                    wait(sp, S.cond_done, g.number - 1)
                    wait(sp, S.resid_ready, g.number - 1)
                sp.dma_start(xin[:, g.parity].rearrange("p s j h -> p s (j h)"), x_g[g.number]).then_inc(x_loaded[g.parity], 16)

            def load_selected(g):
                chosen = [sp.value_load(expert_ids[0:1, bass.ds(g.number * GS + s, 1)], min_val=0, max_val=EXPERTS - 1)
                          for s in range(GS)]
                wait(sp, S.back_full, back_at(g, B_WO) - BACK_FILLS)
                for s in range(GS):
                    sp.dma_start(wsel[:, s, :], merged[bass.ds(chosen[s], 1)].rearrange("e p n -> p (e n)")).then_inc(S.wsel_loaded, 16)

            def store(g):
                sp.wait_ge(taken_k[B_TOK % 2], taken_at(g, B_TOK))
                sp.dma_start(out_g[g.number], tok.rearrange("l (b h) -> l b h", b=GS)).then_inc(S.stored, 16)

            load_x(group(0, 0))
            for b in range(2):
                rows = slice(64 * b, 64 * b + 64)
                sp.dma_start(rot[rows, 0, :], delta_t[b:b + 1, :].to_broadcast([64, BATCH // 2])).then_inc(S.small_loaded, 16)
                sp.dma_start(freq_amp[rows, 0:1], frequencies).then_inc(S.small_loaded, 16)
                sp.dma_start(freq_amp[rows, 1:2], amplitudes).then_inc(S.small_loaded, 16)
            sp.dma_start(col[:, :], columns).then_inc(S.small_loaded, 16)
            sp.dma_start(w_in_s[:, :], w_in).then_inc(S.front_w_loaded, 16)
            sp.dma_start(w_x_s[:, :, :], w_x).then_inc(S.front_w_loaded, 16)
            sp.dma_start(w_dt_s[:, :], w_dt).then_inc(S.front_w_loaded, 16)
            load_x(group(0, 1))
            sp.dma_start(w_out_s, w_out).then_inc(S.fuse_w_loaded, 16)
            sp.dma_start(w_reduce_s, w_reduce).then_inc(S.fuse_w_loaded, 16)
            sp.dma_start(base[:, 0, :], wi).then_inc(S.base_loaded, 16)
            sp.dma_start(base[:, 1, :], wo).then_inc(S.base_loaded, 16)

            def store_merged(e):
                if e < EXPERTS - 1:
                    sp.wait_ge(lora_merged[e % 2], 2 * (e // 2 + 1))
                else:
                    sp.wait_ge(taken_k[0], 1)
                    sp.wait_ge(taken_k[1], 1)
                sp.dma_start(merged[e], staged(e)).then_inc(lora_stored[e % 2] if e < EXPERTS - 1 else S.stored, 16)

            for e in range(EXPERTS):
                if e >= 2:
                    sp.wait_ge(S.lora_full, 2 * (e - 1))
                wi_a, wi_b, wo_a, wo_b = factors(e)
                for dst, common, expert in ((wi_a, common_wi_a, experts_wi_a), (wi_b, common_wi_b, experts_wi_b),
                                            (wo_a, common_wo_a, experts_wo_a), (wo_b, common_wo_b, experts_wo_b)):
                    sp.dma_start(dst[0:RANK, :], common).then_inc(lora_loaded[e % 2], 16)
                    sp.dma_start(dst[RANK:2 * RANK, :], expert[e]).then_inc(lora_loaded[e % 2], 16)
                if e >= 1:
                    store_merged(e - 1)
            store_merged(EXPERTS - 1)
            for dst, src in ((w_glu_s[:, :], w_glu), (w1_s[:, :], w1), (w2_s[:, :], w2), (h1_s[:, :, :], h1),
                             (h2_s[:, :, :], h2), (w3_s[:, :, :], w3)):
                sp.dma_start(dst, src).then_inc(S.back_w_loaded, 16)
            sp.wait_ge(lora_stored[0], 16 * (EXPERTS // 2))
            sp.wait_ge(lora_stored[1], 16 * (EXPERTS // 2 - 1))
            sp.wait_ge(S.stored, 16)

            def period(groups):
                if 1 in groups and not (isinstance(groups[1].number, int) and groups[1].number < 2):
                    load_x(groups[1])
                if -2 in groups:
                    store(groups[-2])
                if 0 in groups:
                    load_selected(groups[0])

            run(sp, period)
            sp.wait_ge(S.stored, 16 * (NG + 1))

        @block.gpsimd
        def _(pool):
            nc.gpsimd.memset(ident[:, :], 0.0).then_inc(S.pick_zero, 1)
            pool.wait_ge(S.pick_zero, 1)
            nc.gpsimd.affine_select(out=ident[:, :], in_=ident[:, :], compare_op=ALU.not_equal, fill=1.0, base=0,
                                    pattern=[[-1, P]], channel_multiplier=1).then_inc(S.ident_ready, 1)
            nc.gpsimd.memset(pick[:, :], 0.0).then_inc(S.pick_step, 1)
            for part in range(3):
                pool.wait_ge(S.pick_step, part + 1)
                nc.gpsimd.affine_select(out=pick[:, :], in_=pick[:, :], compare_op=ALU.not_equal, fill=1.0,
                                        base=-32 * part, pattern=[[-1, 32]], channel_multiplier=1).then_inc(S.pick_step, 1)
            nc.gpsimd.memset(half_power[:, :], -0.5).then_inc(S.consts_ready, 1)

            def norm_power(g):
                wait(pool, S.consts_ready, 1)
                wait(pool, S.var_ready, g.number + 1)
                wait(pool, S.xn_ready, g.number)
                nc.gpsimd.tensor_tensor(rstd[:, :], var_eps[:, :], half_power[:, :], ALU.pow).then_inc(S.rstd_ready, 1)

            def residual(g):
                wait(pool, x_loaded[g.parity], g.turn * 16 + 16)
                wait(pool, S.cond_done, g.number + 1)
                wait(pool, S.back_full, back_at(g, B_RES) - 2 * BACK_FILLS)
                nc.gpsimd.tensor_tensor(resid[:, g.parity], xin[:, g.parity].rearrange("p s j h -> p j s h"),
                                        xc[:, :, :, :].rearrange("p s j h -> p j s h"), ALU.add).then_inc(S.resid_ready, 1)

            def step_sizes(g, d):
                wait(pool, S.log_ready, g.number * 2 + (d + 1))
                wait(pool, S.exp_done, unit_at(g, 16 * d + 15) - UNITS)
                nc.gpsimd.tensor_tensor(delta[:, d], relu_dt[:, :, :], log_dt[:, :, :], ALU.add).then_inc(S.delta_ready, 1)
                wait(pool, S.delta_ready, g.number * 2 + (d + 1))
                wait(pool, S.u_ready, g.number * 2 + 2)
                wait(pool, S.bx_ready, unit_at(g, 16 * d + 15) - UNITS)
                u = (u_f, u_r)[d]
                nc.gpsimd.tensor_tensor(du[:, d], delta[:, d], u[:, g.parity], ALU.mult).then_inc(S.du_ready, 1)

            def unit(g, k):
                d = k // NST
                if k % NST == 0:
                    pool.wait_ge(S.du_ready, g.number * 2 + (d + 1))
                pool.wait_ge(S.b_copied, unit_at(g, k))
                wait(pool, S.states_summed, unit_at(g, k) - RING)
                nc.gpsimd.tensor_tensor(state[:, k % RING], du[:, d],
                                        b_rows[:, k % 2, :].unsqueeze(1).to_broadcast([P, HALVES, GT]),
                                        ALU.mult).then_inc(S.bx_ready, 1)

            def period(groups):
                for k in range(UNITS):
                    g, n = around(groups, k + AHEAD)
                    if g:
                        unit(g, n)
                    if 0 in groups and k == DIR1_SLOT + 5:
                        step_sizes(groups[0], 1)
                    if 1 in groups:
                        if k == COND_SLOT + 2:
                            norm_power(groups[1])
                        if k == RESID_SLOT:
                            residual(groups[1])
                        if k == DIR0_SLOT + 6:
                            step_sizes(groups[1], 0)

            run(pool, period)

        @block.scalar
        def _(act):
            def rotation_tables():
                act.wait_ge(S.small_loaded, 7 * 16)
                act.activation(rot[:, 2, 0:1], freq_amp[:, 1:2], ACT.Ln).then_inc(S.rot_act, 1)
                act.wait_ge(S.rot_act, 1)
                act.activation(rot[:, 3, :], rot[:, 0, :], ACT.Exp, scale=rot[:, 2, 0:1]).then_inc(S.rot_act, 1)
                act.activation(a_neg[:, :, :].rearrange("p h n -> p (h n)"), col[:, COLS["a_log"]:COLS["a_log"] + HALVES * NST],
                               ACT.Exp).then_inc(S.rot_act, 1)
                act.wait_ge(S.rot_dve, 4)
                act.activation(rot[:, 5, :], rot[:, 1, :], ACT.Abs).then_inc(S.rot_act, 1)
                act.wait_ge(S.rot_act, 4)
                act.activation(rot[:, 4, :], rot[:, 1, :], ACT.Sin).then_inc(S.rot_act, 1)
                act.wait_ge(S.consts_ready, 2)
                act.activation(rot[:, 6, :], rot[:, 5, :], ACT.Sin, scale=-1.0, bias=halfpi_col[:, 0:1]).then_inc(S.rot_act, 1)

            def scale_pairs(g):
                wait(act, x_loaded[g.parity], g.turn * 16 + 16)
                wait(act, S.rot_ready, 3)
                wait(act, S.cond_done, g.number)
                for s in range(2):
                    n = bass.ds(g.number * 2 + s, 1)
                    act.activation(scaled[:, s, 0], xin[:, g.parity, s, 0], ACT.Copy, scale=rot[:, 0, n])
                    ins = act.activation(scaled[:, s, 1], xin[:, g.parity, s, 0], ACT.Copy, scale=rot[:, 1, n])
                ins.then_inc(S.scaled_ready, 1)

            def norm_out(g):
                act.wait_ge(S.front_full, front_at(g, F_NORM))
                act.activation(token_order(xnT[:, :]), transposed_order(bank_f[:, :]), ACT.Identity,
                               scale=c("ln_g"), bias=c("ln_b")).then_inc(S.front_taken, 1)

            def conv_start(g, h):
                act.wait_ge(S.front_full, front_at(g, F_XI0 + h))
                wait(act, S.y_taken, g.number * 2 - 2)
                wait(act, S.u_ready, g.number * 2)
                wait(act, S.delta_ready, g.number * 2)
                tap = c("conv_w", h * TAPS + TAPS - 1)
                act.activation(u_f[:, g.parity, h], bank_f[:, :], ACT.Identity, scale=tap, bias=c("conv_b", h))
                act.activation(acc_r[:, h], bank_f[:, :], ACT.Identity, scale=tap, bias=c("conv_b", h)).then_inc(S.conv_init, 1)

            def silu_z(g, h):
                act.wait_ge(S.front_full, front_at(g, F_Z0 + h))
                wait(act, S.gated_ready, g.number * 2 - 2)
                act.activation(z[:, g.parity, h], bank_f[:, :], ACT.Silu).then_inc(S.front_taken, 1)

            def silu_u(g):
                act.wait_ge(S.front_taken, front_at(g, F_XI1))
                act.activation(u_f[:, g.parity], u_f[:, g.parity], ACT.Silu).then_inc(S.u_ready, 1)
                act.activation(u_r[:, g.parity, :, ::-1], acc_r[:, :, :], ACT.Silu).then_inc(S.u_ready, 1)

            def take_dbc(g, d):
                fill = (F_DBC0, F_DBC1)[d]
                act.wait_ge(S.front_full, front_at(g, fill))
                wait(act, S.c_full, unit_at(g, 16 * d + 15) - UNITS)
                act.activation(dtT[:, :], bank_f[0:DTR, :], ACT.Copy)
                act.activation(parts[0:32, d], bank_f[DTR:DTR + 32, :], ACT.Copy).then_inc(S.dt_copied, 1)

            def softplus_in(g, d, h):
                fill = (F_DT00, F_DT10)[d] + h
                act.wait_ge(S.front_full, front_at(g, fill))
                wait(act, S.delta_ready, g.number * 2 + d)
                act.wait_ge(S.u_ready, g.number * 2 + 2)
                act.activation(log_dt[:, h], bank_f[:, :], ACT.Abs, bias=c("dt_b", h)).then_inc(S.abs_ready, 1)
                act.activation(relu_dt[:, h], bank_f[:, :], ACT.Relu, bias=c("dt_b", h)).then_inc(S.front_taken, 1)

            def softplus_out(g, d):
                act.wait_ge(S.abs_ready, g.number * 4 + (2 * d + 2))
                act.activation(log_dt[:, :, :], log_dt[:, :, :], ACT.Exp, scale=-1.0).then_inc(S.exp_ready, 1)
                act.wait_ge(S.exp_ready, g.number * 2 + (d + 1))
                act.activation(log_dt[:, :, :], log_dt[:, :, :], ACT.Ln, bias=one_col[:, 0:1]).then_inc(S.log_ready, 1)

            def copy_b(g, k):
                act.wait_ge(S.b_full, unit_at(g, k))
                wait(act, S.bx_ready, unit_at(g, k) - 2)
                act.activation(b_rows[:, k % 2], bank_b[:, :], ACT.Copy).then_inc(S.b_copied, 1)

            def decays(g, k):
                d, n = k // NST, k % NST
                if n == 0:
                    act.wait_ge(S.delta_ready, g.number * 2 + (d + 1))
                wait(act, S.scanned, unit_at(g, k) - DECAYS)
                for h in range(HALVES):
                    ins = act.activation(decay[:, k % DECAYS, h, :, 1:], delta[:, d, h].rearrange("p (b t) -> p b t", b=GS)[:, :, 1:],
                                         ACT.Exp, scale=a_neg[:, h, n:n + 1])
                ins.then_inc(S.exp_done, 1)

            def take(g, fill, dst, func, **kw):
                act.wait_ge(S.back_full, back_at(g, fill))
                act.activation(dst, bank_k[fill % 2][:, :], func, **kw).then_inc(taken_k[fill % 2], 1)

            def pair_take(g, k, slots, fills, dst, func, scale=None):
                for j in range(2):
                    f = 2 * slots.index(k) + j
                    kw = {} if scale is None else {"scale": c(scale, f)}
                    take(g, fills[f], dst[:, f % dst.shape[1]], func, **kw)

            def back(g, k):
                if k == OUT_SLOT + 1:
                    take(g, B_OUT, gy[:, :], ACT.Gelu, bias=c("reduce_b"))
                if k == GLU_SLOT + 1:
                    wait(act, S.hb_ready, 1)
                    take(g, B_GLU0, glu_a[:, :], ACT.Identity, scale=0.5, bias=hb[:, 0:1])
                    take(g, B_GLU1, glu_t[:, :], ACT.Tanh, scale=0.5, bias=hb[:, 1:2])
                if k - 1 in HID_SLOTS:
                    pair_take(g, k - 1, HID_SLOTS, B_HID, hidA, ACT.Relu)
                if k == WO_SLOT + 1:
                    take(g, B_WO, cT[:, :], ACT.Copy)
                if k - 1 in GATE_SLOTS:
                    if k - 1 == GATE_SLOTS[0]:
                        act.wait_ge(S.stored, g.number * 16 + 16)
                    else:
                        for f in range(2):
                            act.wait_ge(taken_k[B_UP[f] % 2], taken_at(g, B_UP[f]))
                    pair_take(g, k - 1, GATE_SLOTS, B_GATE, gate, ACT.Silu, "w1_s")
                if k - 2 in H1_SLOTS:
                    pair_take(g, k - 2, H1_SLOTS, B_H1, hidA, ACT.Gelu, "h1_s")
                if k - 2 in H2_SLOTS:
                    pair_take(g, k - 2, H2_SLOTS, B_H2, hidB, ACT.Gelu, "h2_s")
                if k == TOK_SLOT + 1:
                    take(g, B_TOK, tok, ACT.Copy)

            def copy_y(g, d):
                act.wait_ge(S.states_summed, unit_at(g, NST * d + NST - 1))
                wait(act, S.gated_ready, g.number * 2 + d)
                act.activation(y_rows[:, :, :], bank_y[:, :, :], ACT.Copy).then_inc(S.y_copied, 1)

            def front(g, k):
                if k == COND_SLOT:
                    scale_pairs(g)
                if k == NORM_SLOT + 1:
                    norm_out(g)
                if k == XI_SLOTS[0] + 1:
                    conv_start(g, 0)
                if k == XI_SLOTS[1] + 1:
                    conv_start(g, 1)
                if k == Z_SLOTS[0] + 1:
                    silu_z(g, 0)
                    silu_u(g)
                if k == Z_SLOTS[1] + 1:
                    silu_z(g, 1)

            def steps(g, k, d):
                if k == 1:
                    take_dbc(g, d)
                if k == 3:
                    softplus_in(g, d, 0)
                if k == 4:
                    softplus_in(g, d, 1)
                    softplus_out(g, d)

            def period(groups):
                for k in range(UNITS):
                    g, n = around(groups, k + AHEAD)
                    if g:
                        copy_b(g, n)
                        decays(g, n)
                    for d in range(2):
                        g, n = around(groups, k - Y_SLOTS[d])
                        if g and n == 0:
                            copy_y(g, d)
                    if 0 in groups:
                        steps(groups[0], k - DIR1_SLOT, 1)
                    if 1 in groups:
                        front(groups[1], k)
                        steps(groups[1], k - DIR0_SLOT, 0)
                    for j in (-2, -1):
                        if j in groups:
                            back(groups[j], k - j * UNITS)

            rotation_tables()
            act.wait_ge(S.decay_zero, 1)
            act.wait_ge(S.a_ready, 1)
            run(act, period)

        @block.vector
        def _(dve):
            def rotation_tables():
                dve.memset(one_col[:, :], 1.0)
                dve.memset(halfpi_col[:, :], PI / 2).then_inc(S.consts_ready, 1)
                dve.memset(decay[:, :, :, :, :].rearrange("p a h b t -> p (a h b t)"), 0.0).then_inc(S.decay_zero, 1)
                dve.wait_ge(S.small_loaded, 7 * 16)
                dve.tensor_scalar(hb[:, :], col[:, COLS["glu_b"]:COLS["glu_b"] + 2], 0.5, None, ALU.mult).then_inc(S.hb_ready, 1)
                turn_hi = 6.28125
                turn_lo = 2 * PI - turn_hi
                big = 1.5 * 2.0 ** 23
                ang, turns, red = rot[:, 4, :], rot[:, 5, :], rot[:, 1, :]
                dve.tensor_scalar(ang, rot[:, 0, :], freq_amp[:, 0:1], None, ALU.mult).then_inc(S.rot_dve, 1)
                dve.wait_ge(S.rot_dve, 1)
                dve.tensor_scalar(turns, ang, 1.0 / (2 * PI), big, ALU.mult, ALU.add).then_inc(S.rot_ready, 1)
                dve.wait_ge(S.rot_ready, 1)
                dve.tensor_scalar(turns, turns, big, None, ALU.subtract).then_inc(S.rot_dve, 1)
                dve.wait_ge(S.rot_dve, 2)
                dve.scalar_tensor_tensor(rot[:, 7, :], turns, -turn_hi, ang, ALU.mult, ALU.add).then_inc(S.rot_dve, 1)
                dve.wait_ge(S.rot_dve, 3)
                dve.scalar_tensor_tensor(red, turns, -turn_lo, rot[:, 7, :], ALU.mult, ALU.add).then_inc(S.rot_ready, 1)
                dve.wait_ge(S.rot_ready, 2)
                dve.tensor_scalar(red, red, 3.1415925, -3.1415925, ALU.min, ALU.max).then_inc(S.rot_dve, 1)
                dve.wait_ge(S.rot_act, 6)
                dve.tensor_tensor(rot[:, 0, :], rot[:, 3, :], rot[:, 6, :], ALU.mult)
                dve.tensor_tensor(rot[:, 1, :], rot[:, 3, :], rot[:, 4, :], ALU.mult)
                dve.scalar_tensor_tensor(rot[:, 2, :], rot[:, 3, :], -1.0, rot[:, 4, :], ALU.mult, ALU.mult).then_inc(S.rot_ready, 1)
                dve.tensor_scalar(a_neg[:, :, :], a_neg[:, :, :], -1.0, None, ALU.mult).then_inc(S.a_ready, 1)
                dve.wait_ge(S.rot_ready, 3)

            def rotate(g):
                dve.wait_ge(S.scaled_ready, g.number + 1)
                wait(dve, S.resid_ready, g.number)
                wait(dve, S.xn_ready, g.number)
                for s in range(2):
                    n = bass.ds(g.number * 2 + s, 1)
                    x1 = xin[:, g.parity, s, 1]
                    dve.scalar_tensor_tensor(xc[:, s, 0], x1, rot[:, 2, n], scaled[:, s, 0], ALU.mult, ALU.add)
                    ins = dve.scalar_tensor_tensor(xc[:, s, 1], x1, rot[:, 0, n], scaled[:, s, 1], ALU.mult, ALU.add)
                ins.then_inc(S.cond_done, 1)
                dve.wait_ge(S.cond_done, g.number + 1)
                for t in range(GS):
                    ins = dve.bn_stats(stats[:, t], xc[:, t // 2, t % 2])
                ins.then_inc(S.stats_done, 1)
                dve.wait_ge(S.small_loaded, 7 * 16)
                dve.wait_ge(S.stats_done, g.number + 1)
                for t in range(GS):
                    ins = dve.bn_aggr(moments[:, t], stats[:, t])
                ins.then_inc(S.aggr_done, 1)
                dve.wait_ge(S.aggr_done, g.number + 1)
                wait(dve, S.rstd_ready, g.number)
                dve.tensor_scalar(var_eps[:, :], moments[:, :, 1], LN_EPS, None, ALU.add).then_inc(S.var_ready, 1)

            def normalise(g):
                dve.wait_ge(S.rstd_ready, g.number + 1)
                wait(dve, S.front_full, front_at(g, F_NORM) - FRONT_FILLS)
                for t in range(GS):
                    ins = dve.tensor_scalar(xn[:, t // 2, t % 2], xc[:, t // 2, t % 2], moments[:, t, 0:1], rstd[:, t:t + 1],
                                            ALU.subtract, ALU.mult)
                ins.then_inc(S.xn_ready, 1)

            def conv_taps(g, h):
                dve.wait_ge(S.conv_init, g.number * 2 + (h + 1))
                xi = bank_f[:, :].rearrange("p (b t) -> p b t", b=GS)
                fwd = u_f[:, g.parity, h].rearrange("p (b t) -> p b t", b=GS)
                rev = acc_r[:, h].rearrange("p (b t) -> p b t", b=GS)
                for m in range(1, TAPS):
                    tap = c("conv_w", h * TAPS + TAPS - 1 - m)
                    if m > 1:
                        dve.wait_ge(S.conv_tap, g.number * 8 + (4 * h + 2 * (m - 1) - 1))
                    ins = dve.scalar_tensor_tensor(fwd[:, :, m:], xi[:, :, :LEN - m], tap, fwd[:, :, m:], ALU.mult, ALU.add)
                    if m < TAPS - 1:
                        ins.then_inc(S.conv_tap, 1)
                        dve.wait_ge(S.conv_tap, g.number * 8 + (4 * h + 2 * (m - 1))) if m > 1 else None
                    else:
                        dve.wait_ge(S.conv_tap, g.number * 8 + (4 * h + 4))
                    ins = dve.scalar_tensor_tensor(rev[:, :, :LEN - m], xi[:, :, m:], tap, rev[:, :, :LEN - m], ALU.mult, ALU.add)
                    ins.then_inc(S.conv_tap if m < TAPS - 1 else S.front_taken, 1)

            def split_rows(g, d):
                dve.wait_ge(S.dt_copied, g.number * 2 + (d + 1))
                dve.tensor_tensor(rest[32:64, :], bank_f[DTR:DTR + 32, :], parts[0:32, d], ALU.subtract).then_inc(S.front_taken, 1)
                dve.wait_ge(S.front_taken, front_at(g, (F_DBC0, F_DBC1)[d]))
                dve.tensor_copy(parts[32:64, d], rest[32:64, :]).then_inc(S.mid_ready, 1)
                dve.wait_ge(S.mid_ready, g.number * 2 + (d + 1))
                dve.tensor_tensor(parts[64:96, d], rest[32:64, :], parts[32:64, d], ALU.subtract).then_inc(S.parts_ready, 1)

            def unit(g, k):
                dve.wait_ge(S.exp_done, unit_at(g, k))
                dve.wait_ge(S.bx_ready, unit_at(g, k))
                st = state[:, k % RING].rearrange("p h t -> p (h t)")
                dve.tensor_tensor_scan(st, decay[:, k % DECAYS].rearrange("p h b t -> p (h b t)"), st, 0.0,
                                       ALU.mult, ALU.add).then_inc(S.scanned, 1)

            def weigh(g, k):
                dve.wait_ge(S.scanned, unit_at(g, k))
                dve.wait_ge(S.c_full, unit_at(g, k))
                dve.tensor_tensor(state[:, k % RING], state[:, k % RING],
                                  bank_c[k % 2][:, :].unsqueeze(1).to_broadcast([P, HALVES, GT]), ALU.mult).then_inc(S.product_done, 1)

            def take_y(g, d):
                dve.wait_ge(S.y_turned, g.number * 2 + (d + 1))
                wait(dve, S.gated_ready, g.number * 2 + d)
                u = (u_f, u_r)[d]
                for h in range(HALVES):
                    dst = ysum[:, h, :] if d == 0 else ysum[:, h, ::-1]
                    ins = dve.scalar_tensor_tensor(dst, u[:, g.parity, h], c("skip_d", h), bank_y[:, h], ALU.mult, ALU.add)
                ins.then_inc(S.y_taken, 1)
                dve.wait_ge(S.y_taken, g.number * 2 + (d + 1))
                wait(dve, S.back_full, back_at(g, B_OUT) - BACK_FILLS)
                dve.tensor_tensor(gated[:, d], ysum[:, :, :], z[:, g.parity], ALU.mult).then_inc(S.gated_ready, 1)

            def back(g, k):
                if k == RES_SLOT + 1:
                    dve.wait_ge(taken_k[0], taken_at(g, B_GLU1))
                    dve.wait_ge(taken_k[1], taken_at(g, B_GLU0))
                    dve.scalar_tensor_tensor(x1T[:, :], glu_t[:, :], 1.0, glu_a[:, :], ALU.add, ALU.mult).then_inc(S.x1_ready, 1)
                    dve.wait_ge(S.x1_ready, g.number + 1)
                    dve.wait_ge(S.back_full, back_at(g, B_RES))
                    dve.tensor_tensor(token_order(x1T[:, :]), token_order(x1T[:, :]), transposed_order(bank_k[B_RES % 2][:, :]),
                                      ALU.add).then_inc(taken_k[B_RES % 2], 1)
                if k - 1 in UP_SLOTS:
                    for j in range(2):
                        f = 2 * UP_SLOTS.index(k - 1) + j
                        dve.wait_ge(S.back_full, back_at(g, B_UP[f]))
                        dve.wait_ge(taken_k[B_GATE[f] % 2], taken_at(g, B_GATE[f]))
                        dve.scalar_tensor_tensor(hidB[:, f], bank_k[B_UP[f] % 2][:, :], c("w2_s", f), gate[:, f % 2],
                                                 ALU.mult, ALU.mult).then_inc(taken_k[B_UP[f] % 2], 1)
                if k == W3_SLOT + 1:
                    dve.wait_ge(S.back_full, back_at(g, B_W3))
                    dve.scalar_tensor_tensor(oT[:, :], bank_k[B_W3 % 2][:, :], c("w3_s"), x1T[:, :],
                                             ALU.mult, ALU.add).then_inc(taken_k[B_W3 % 2], 1)

            def merge(e):
                if e == 0:
                    dve.wait_ge(S.base_loaded, 32)
                    dve.wait_ge(S.fused_full, 1)
                    dve.tensor_copy(w_fused[:, :, :, :].rearrange("p d h o -> p (d h o)"), bank_k[0][:, :]).then_inc(S.fused_ready, 1)
                for part in range(2):
                    dve.wait_ge(S.lora_full, 2 * e + part + 1)
                    if e >= 2:
                        dve.wait_ge(lora_stored[e % 2], 16 * (e // 2))
                    dve.scalar_tensor_tensor(staged(e)[:, part * FF:(part + 1) * FF], bank_k[part][:, :], LORA_ALPHA, base[:, part],
                                             ALU.mult, ALU.add).then_inc(lora_merged[e % 2] if e < EXPERTS - 1 else taken_k[part], 1)

            def front(g, k):
                if k == COND_SLOT + 1:
                    rotate(g)
                if k == COND_SLOT + 3:
                    normalise(g)
                if k == XI_SLOTS[0] + 1:
                    conv_taps(g, 0)
                if k == XI_SLOTS[1] + 1:
                    conv_taps(g, 1)
                if k == DIR0_SLOT + 1:
                    split_rows(g, 0)

            def period(groups):
                for k in range(UNITS):
                    if 0 in groups:
                        unit(groups[0], k)
                    g, n = around(groups, k - 1)
                    if g:
                        weigh(g, n)
                    if 0 in groups and k == DIR1_SLOT + 1:
                        split_rows(groups[0], 1)
                    for d in range(2):
                        g, n = around(groups, k - Y_SLOTS[d] - 1)
                        if g and n == 0:
                            take_y(g, d)
                    if 1 in groups:
                        front(groups[1], k)
                    for j in (-2, -1):
                        if j in groups:
                            back(groups[j], k - j * UNITS)
                    if 0 in groups and -1 not in groups and k in MERGE_SLOTS:
                        merge(MERGE_SLOTS.index(k))

            rotation_tables()
            run(dve, period)

        @block.tensor
        def _(pe):
            def fill_front(g, fill):
                wait(pe, S.front_taken, front_at(g, fill) - 1)

            def transpose_norm(g):
                wait(pe, S.ident_ready, 1)
                pe.wait_ge(S.xn_ready, g.number + 1)
                fill_front(g, F_NORM)
                for t in range(GS):
                    s, j = t // 2, t % 2
                    at = (2 * j + s) * P
                    ins = pe.transpose(bank_f[:, at:at + P], xn[:, s, j], ident[:, :])
                ins.then_inc(S.front_full, 1)

            def project_in(g, fill):
                m = fill - F_XI0
                wait(pe, S.front_w_loaded, 48)
                fill_front(g, fill)
                pe.matmul(bank_f[:, :], w_in_s[:, m * P:(m + 1) * P], xnT[:, :], start=True, stop=True).then_inc(S.front_full, 1)

            def project_x(g, d):
                fill = (F_DBC0, F_DBC1)[d]
                fill_front(g, fill)
                pe.wait_ge(S.u_ready, g.number * 2 + 2)
                u = (u_f, u_r)[d]
                for h in range(HALVES):
                    ins = pe.matmul(bank_f[0:DTR + 2 * NST, :], w_x_s[:, h], u[:, g.parity, h], start=(h == 0), stop=(h == HALVES - 1))
                ins.then_inc(S.front_full, 1)

            def project_dt(g, d, h):
                fill = (F_DT00, F_DT10)[d] + h
                fill_front(g, fill)
                pe.wait_ge(S.dt_copied, g.number * 2 + (d + 1))
                pe.matmul(bank_f[:, :], w_dt_s[:, h * P:(h + 1) * P], dtT[:, :], start=True, stop=True).then_inc(S.front_full, 1)

            def spread_b(g, k):
                d, n = k // NST, k % NST
                if n == 0:
                    pe.wait_ge(S.parts_ready, g.number * 2 + (d + 1))
                wait(pe, S.b_copied, unit_at(g, k) - 1)
                pe.matmul(bank_b[:, :], pick[:, n:n + 1].to_broadcast([96, P]), parts[:, d], start=True, stop=True).then_inc(S.b_full, 1)

            def spread_c(g, k):
                d, n = k // NST, k % NST
                wait(pe, S.product_done, unit_at(g, k) - 2)
                pe.matmul(bank_c[k % 2][:, :], pick[:, NST + n:NST + n + 1].to_broadcast([96, P]), parts[:, d], start=True, stop=True).then_inc(S.c_full, 1)

            def sum_states(g, k):
                d, n = k // NST, k % NST
                pe.wait_ge(S.product_done, unit_at(g, k))
                if n == 0:
                    wait(pe, S.y_taken, g.number * 2 + d)
                for h in range(HALVES):
                    for s in range(GS):
                        ins = pe.matmul(bank_y[:, h, s * P:(s + 1) * P], state[:, k % RING, h, s * LEN:(s + 1) * LEN], ident[:, :],
                                        start=(n == 0 and s == 0), stop=(n == NST - 1), is_transpose=True, skip_group_check=True)
                ins.then_inc(S.states_summed, 1)

            def turn_y(g, d):
                pe.wait_ge(S.y_copied, g.number * 2 + (d + 1))
                for h in range(HALVES):
                    for s in range(GS):
                        ins = pe.transpose(bank_y[:, h, s * LEN:(s + 1) * LEN], y_rows[:, h, s * P:(s + 1) * P], ident[:, :])
                ins.then_inc(S.y_turned, 1)

            def fill_back(g, fill, *sources):
                for bank in range(2):
                    fills = [f for f in (fill - 2, *sources) if f % 2 == bank]
                    if fills:
                        wait(pe, taken_k[bank], taken_at(g, max(fills)))

            def back(g, k):
                if k == OUT_SLOT:
                    wait(pe, S.fused_ready, 1)
                    pe.wait_ge(S.gated_ready, g.number * 2 + 2)
                    fill_back(g, B_OUT)
                    for d in range(2):
                        for h in range(HALVES):
                            ins = pe.matmul(bank_k[0][:, :], w_fused[:, d, h], gated[:, d, h], start=(d == 0 and h == 0),
                                            stop=(d == 1 and h == HALVES - 1))
                    ins.then_inc(S.back_full, 1)
                if k == GLU_SLOT:
                    wait(pe, S.back_w_loaded, 6 * 16)
                    for m in range(2):
                        fill_back(g, B_GLU0 + m, B_OUT)
                        pe.matmul(bank_k[(B_GLU0 + m) % 2][:, :], w_glu_s[:, m * P:(m + 1) * P], gy[:, :], start=True,
                                  stop=True).then_inc(S.back_full, 1)
                if k == RES_SLOT:
                    fill_back(g, B_RES)
                    pe.wait_ge(S.resid_ready, g.number + 1)
                    for t in range(GS):
                        ins = pe.transpose(bank_k[B_RES % 2][:, t * P:(t + 1) * P], resid[:, g.parity, t // 2, t % 2], ident[:, :])
                    ins.then_inc(S.back_full, 1)
                if k in HID_SLOTS:
                    pe.wait_ge(S.wsel_loaded, g.number * (16 * GS) + 16 * GS)
                    for j in range(2):
                        f = 2 * HID_SLOTS.index(k) + j
                        fill_back(g, B_HID[f], B_RES)
                        for s in range(GS):
                            ins = pe.matmul(bank_k[f % 2][:, s * LEN:(s + 1) * LEN], wsel[:, s, f * P:(f + 1) * P],
                                            x1T[:, s * LEN:(s + 1) * LEN], start=True, stop=True)
                        ins.then_inc(S.back_full, 1)
                if k == WO_SLOT:
                    fill_back(g, B_WO, *B_HID)
                    for s in range(GS):
                        for f in range(FC):
                            ins = pe.matmul(bank_k[B_WO % 2][:, s * LEN:(s + 1) * LEN], wsel[:, s, FF + f * HID:FF + (f + 1) * HID],
                                            hidA[:, f, s * LEN:(s + 1) * LEN], start=(f == 0), stop=(f == FC - 1))
                    ins.then_inc(S.back_full, 1)
                for slots, fills, w in ((GATE_SLOTS, B_GATE, w1_s), (UP_SLOTS, B_UP, w2_s)):
                    if k in slots:
                        for j in range(2):
                            f = 2 * slots.index(k) + j
                            fill_back(g, fills[f], B_WO)
                            pe.matmul(bank_k[fills[f] % 2][:, :], w[:, f * P:(f + 1) * P], cT[:, :], start=True,
                                      stop=True).then_inc(S.back_full, 1)
                for slots, fills, w, src, before in ((H1_SLOTS, B_H1, h1_s, hidB, B_UP), (H2_SLOTS, B_H2, h2_s, hidA, B_H1)):
                    if k in slots or k - 1 in slots:
                        f = 2 * slots.index(k) if k in slots else 2 * slots.index(k - 1) + 1
                        fill_back(g, fills[f], *before)
                        for q in range(FC):
                            ins = pe.matmul(bank_k[fills[f] % 2][:, :], w[:, q, f * P:(f + 1) * P], src[:, q],
                                            start=(q == 0), stop=(q == FC - 1))
                        ins.then_inc(S.back_full, 1)
                if k == W3_SLOT:
                    fill_back(g, B_W3, *B_H2)
                    for q in range(FC):
                        ins = pe.matmul(bank_k[B_W3 % 2][:, :], w3_s[:, q], hidB[:, q], start=(q == 0), stop=(q == FC - 1))
                    ins.then_inc(S.back_full, 1)
                if k == TOK_SLOT:
                    fill_back(g, B_TOK, B_W3)
                    for s in range(GS):
                        ins = pe.transpose(bank_k[B_TOK % 2][:, s * P:(s + 1) * P], oT[:, s * LEN:(s + 1) * LEN], ident[:, :])
                    ins.then_inc(S.back_full, 1)

            def fuse_out():
                pe.wait_ge(S.fuse_w_loaded, 32)
                for d in range(2):
                    for h in range(HALVES):
                        at = (d * HALVES + h) * HID
                        ins = pe.matmul(bank_k[0][:, at:at + HID], w_out_s[:, h * P:(h + 1) * P], w_reduce_s[:, d], start=True, stop=True)
                ins.then_inc(S.fused_full, 1)

            def merge(e):
                wi_a, wi_b, wo_a, wo_b = factors(e)
                pe.wait_ge(lora_loaded[e % 2], 16 * 8 * (e // 2 + 1))
                if e == 0:
                    pe.wait_ge(S.fused_ready, 1)
                else:
                    pe.wait_ge(lora_merged[(e - 1) % 2], 2 * ((e - 1) // 2 + 1))
                pe.matmul(bank_k[0][:, :], wi_a, wi_b, start=True, stop=True).then_inc(S.lora_full, 1)
                for f in range(FC):
                    ins = pe.matmul(bank_k[1][:, f * HID:(f + 1) * HID], wo_a[:, f * P:(f + 1) * P], wo_b, start=True, stop=True)
                ins.then_inc(S.lora_full, 1)

            def front(g, k):
                if k == NORM_SLOT:
                    transpose_norm(g)
                for slots, fills in ((XI_SLOTS, (F_XI0, F_XI1)), (Z_SLOTS, (F_Z0, F_Z1))):
                    if k in slots:
                        project_in(g, fills[slots.index(k)])

            def steps(g, k, d):
                if k == 0:
                    project_x(g, d)
                if k == 2:
                    project_dt(g, d, 0)
                if k == 3:
                    project_dt(g, d, 1)

            def period(groups):
                for k in range(UNITS):
                    g, n = around(groups, k)
                    if g:
                        spread_c(g, n)
                    g, n = around(groups, k + AHEAD + 1)
                    if g:
                        spread_b(g, n)
                    for d in range(2):
                        g, n = around(groups, k - Y_SLOTS[d])
                        if g and n == 0:
                            turn_y(g, d)
                    g, n = around(groups, k - SUM_LAG)
                    if g and n % NST >= HELD:
                        for m in range(n - HELD if n % NST == HELD else n, n + 1):
                            sum_states(g, m)
                    if 0 in groups:
                        steps(groups[0], k - DIR1_SLOT, 1)
                    if 1 in groups:
                        front(groups[1], k)
                        steps(groups[1], k - DIR0_SLOT, 0)
                    for j in (-2, -1):
                        if j in groups:
                            back(groups[j], k - j * UNITS)
                    if 0 in groups and -1 not in groups and k in MERGE_SLOTS:
                        if k == MERGE_SLOTS[0]:
                            fuse_out()
                        merge(MERGE_SLOTS.index(k))

            pe.wait_ge(S.pick_step, 4)
            run(pe, period)


DIR1_SLOT = 0
COND_SLOT = 3
NORM_SLOT = 7
XI_SLOTS = (9, 11)
RESID_SLOT = 12
Z_SLOTS = (15, 18)
DIR0_SLOT = 20
AHEAD = 3
SUM_LAG, HELD = 2, 3
Y_SLOTS = (19, 35)
OUT_SLOT = UNITS + 5
GLU_SLOT = UNITS + 7
RES_SLOT = UNITS + 8
HID_SLOTS = (UNITS + 10, UNITS + 11)
WO_SLOT = UNITS + 13
GATE_SLOTS = (UNITS + 15, UNITS + 18)
UP_SLOTS = (UNITS + 17, UNITS + 20)
H1_SLOTS = (UNITS + 21, UNITS + 24)
H2_SLOTS = (UNITS + 27, UNITS + 30)
W3_SLOT = UNITS + 33
TOK_SLOT = UNITS + 34
MERGE_SLOTS = tuple(range(6, 6 + 2 * EXPERTS, 2))


def kernel(**inputs):
    import concourse.bacc as _bacc
    from concourse.bass_utils import run_bass_kernel_spmd as _run

    def host(name):
        return np.asarray(inputs[name])

    def halves(a):
        return a.reshape(HALVES, P, -1).transpose(1, 0, 2).reshape(P, -1)

    def chunked(a):
        return a.reshape(-1, P, a.shape[1]).transpose(1, 0, 2)

    attn, cond2, ffn = "L0_attn_", "L0_cond2_", "L0_ffn_"
    columns = np.concatenate([
        halves(host(attn + "conv_w").reshape(DI, TAPS)), halves(host(attn + "conv_b")), halves(host(attn + "dt_proj_b")),
        halves(host(attn + "D")), halves(host(attn + "A_log")), host(attn + "ln_g").reshape(P, 1), host(attn + "ln_b").reshape(P, 1),
        host(attn + "dim_reduce_b").reshape(P, 1), halves(host(attn + "glu_b")),
        host(ffn + "w1_s").reshape(FC, P).T, host(ffn + "w2_s").reshape(FC, P).T, host(ffn + "h1_s").reshape(FC, P).T,
        host(ffn + "h2_s").reshape(FC, P).T, host(ffn + "w3_s").reshape(P, 1)], axis=1)
    arrays = {
        "x": host("x"), "delta_t": host("condB_deltat").reshape(BATCH // 2, 2).T, "expert_ids": host("itok_B_0_7").reshape(1, BATCH),
        "amplitudes": host("L0_cond_amplitudes").reshape(-1, 1), "frequencies": host("L0_cond_frequencies").reshape(-1, 1),
        "columns": columns,
        "w_in": host(attn + "in_proj_w").T, "w_x": chunked(host(attn + "x_proj_w").T), "w_dt": host(attn + "dt_proj_w").T,
        "w_out": host(attn + "out_proj_w"), "w_reduce": chunked(host(attn + "dim_reduce_w").T), "w_glu": host(attn + "glu_w").T,
        "wi": host(cond2 + "wi").T, "wo": chunked(host(cond2 + "wo").T).reshape(P, FF),
        "common_wi_a": host(cond2 + "common_wi_a"), "common_wi_b": host(cond2 + "common_wi_b").T,
        "common_wo_a": host(cond2 + "common_wo_a"), "common_wo_b": host(cond2 + "common_wo_b").T,
        "experts_wi_a": host(cond2 + "experts_wi_a"), "experts_wi_b": host(cond2 + "experts_wi_b").transpose(0, 2, 1),
        "experts_wo_a": host(cond2 + "experts_wo_a"), "experts_wo_b": host(cond2 + "experts_wo_b").transpose(0, 2, 1),
        "w1": host(ffn + "w1_w").T, "w2": host(ffn + "w2_w").T, "h1": chunked(host(ffn + "h1_w").T),
        "h2": chunked(host(ffn + "h2_w").T), "w3": chunked(host(ffn + "w3_w").T),
    }
    arrays = {f"in_{k}": np.ascontiguousarray(v) for k, v in arrays.items()}
    nc = _bacc.Bacc("TRN2", target_bir_lowering=False, num_devices=1)
    args = [nc.dram_tensor(k, v.shape, mybir.dt.from_np(v.dtype), kind="ExternalInput").ap() for k, v in arrays.items()]
    args.append(nc.dram_tensor("merged", (EXPERTS, P, 2 * FF), F32, kind="Internal").ap())
    args.append(nc.dram_tensor("out", (BATCH, LEN, HID), F32, kind="ExternalOutput").ap())
    build(nc, *args)
    r = _run(nc, [arrays], core_ids=[0])
    return r.results[0]["out"]
```

```python
from collections import namedtuple
from contextlib import ExitStack

import numpy as np

import concourse.bass as bass
from concourse import mybir

F32 = mybir.dt.float32
BF16 = mybir.dt.bfloat16
I32 = mybir.dt.int32
ALU = mybir.AluOpType
ACT = mybir.ActivationFunctionType

P = 128
BATCH, LEN, HID = 32, 128, 128
DI, NST, TAPS, DTR = 256, 16, 4, 64
EXPERTS, RANK, FF = 8, 16, 512
LN_EPS, LORA_ALPHA = 1e-5, 2.0

GS = 4
NG = BATCH // GS
GT = GS * LEN
HALVES = DI // P
FC = FF // P
UNITS = 2 * NST
RING = 8
DECAYS = 4
ROWS = 4

COLS = {}
_at = 0
for _name, _n in (("conv_w", HALVES * TAPS), ("conv_b", HALVES), ("dt_b", HALVES), ("skip_d", HALVES),
                  ("a_log", HALVES * NST), ("ln_g", 1), ("ln_b", 1), ("reduce_b", 1), ("glu_b", 2),
                  ("w1_s", FC), ("w2_s", FC), ("h1_s", FC), ("h2_s", FC), ("w3_s", 1)):
    COLS[_name] = _at
    _at += _n
NCOLS = _at

(F_NORM, F_XI0, F_XI1, F_Z0, F_Z1, F_DBC0, F_DT00, F_DT01, F_DBC1, F_DT10, F_DT11) = range(11)
FRONT_FILLS = 11
FRONT_BANK_FILLS = ((FRONT_FILLS + 1) // 2, FRONT_FILLS // 2)
B_OUT, B_GLU0, B_GLU1, B_RES = range(4)
B_HID, B_WO = range(4, 8), 8
B_GATE = range(9, 13)
B_UP = range(13, 17)
B_H1, B_H2, B_W3, B_TOK = range(17, 21), range(21, 25), 25, 26
BACK_FILLS = 27
BANK_FILLS = ((BACK_FILLS + 1) // 2, BACK_FILLS // 2)

EXP_LN, SILU, GELU = "natural_log_exp_and_others", "silu_and_others", "gelu_and_others"

Group = namedtuple("Group", "number parity turn")


def group(i, c):
    return Group(i * 2 + c, c % 2, i + c // 2)


def wait(eng, signal, value):
    if isinstance(value, int) and value <= 0:
        return
    eng.wait_ge(signal, value)


def build(nc, x, delta_t, expert_ids, amplitudes, frequencies, columns, w_in, w_x, w_dt, w_out, w_reduce, w_glu,
          wi, wo, common_wi_a, common_wi_b, common_wo_a, common_wo_b,
          experts_wi_a, experts_wi_b, experts_wo_a, experts_wo_b, w1, w2, h1, h2, w3, merged, b_store, out):
    PI = float(np.pi)
    ctx = ExitStack()
    with ctx:
        def sb(name, shape, dt=F32):
            return ctx.enter_context(nc.sbuf_tensor(name, shape, dt))

        def sem(name):
            return ctx.enter_context(nc.semaphore(name))

        col = sb("col", [P, NCOLS])
        w_in_s = sb("w_in_s", [P, 2 * DI])
        w_x_s = sb("w_x_s", [P, HALVES, DTR + 2 * NST])
        w_dt_s = sb("w_dt_s", [DTR, DI])
        w_fused = sb("w_fused", [P, 2, HALVES, HID])
        w_glu_s = sb("w_glu_s", [P, 2 * HID])
        w1_s = sb("w1_s", [P, FF])
        w2_s = sb("w2_s", [P, FF])
        h1_s = sb("h1_s", [P, FC, FF])
        h2_s = sb("h2_s", [P, FC, FF])
        w3_s = sb("w3_s", [P, FC, HID])
        ident = sb("ident", [P, P])
        pick = sb("pick", [96, 32], BF16)
        a_neg = sb("a_neg", [P, HALVES, NST])
        hb = sb("hb", [P, 2])
        rot = sb("rot", [P, 8, BATCH // 2])
        half_power = sb("half_power", [P, GS])
        one_col = sb("one_col", [P, 1])
        halfpi_col = sb("halfpi_col", [P, 1])
        freq_amp = sb("freq_amp", [P, 2])

        xin = sb("xin", [P, 2, 2, 2, HID])
        scaled = sb("scaled", [P, 2, 2, HID])
        xc = sb("xc", [P, 2, 2, HID])
        xn = scaled
        stats = sb("stats", [P, GS, 6])
        moments = sb("moments", [P, GS, 2])
        var_eps = sb("var_eps", [P, GS])
        rstd = sb("rstd", [P, GS])
        resid = sb("resid", [P, 2, 2, 2, HID])
        xnT = sb("xnT", [P, GT])
        u_f = sb("u_f", [P, 2, HALVES, GT])
        u_r = sb("u_r", [P, 2, HALVES, GT])
        z = sb("z", [P, 2, HALVES, GT])
        dbc = sb("dbc", [DTR + 2 * NST, GT])
        parts = sb("parts", [96, 2, GT], BF16)
        rest = sb("rest", [64, GT])
        relu_dt = sb("relu_dt", [P, HALVES, GT])
        acc_r = relu_dt
        log_dt = sb("log_dt", [P, HALVES, GT])
        delta = sb("delta", [P, 2, HALVES, GT])
        du = sb("du", [P, 2, HALVES, GT])

        decay = sb("decay", [P, DECAYS, HALVES, GS, LEN])
        b_rows = sb("b_rows", [P, ROWS, GT])
        state = sb("state", [P, RING, HALVES, GT])

        ysum = sb("ysum", [P, HALVES, GT])
        y_rows = ysum
        gated = sb("gated", [P, 2, HALVES, GT])
        gy = sb("gy", [P, GT])
        glu_a = sb("glu_a", [P, GT])
        glu_t = sb("glu_t", [P, GT])
        x1T = sb("x1T", [P, GT])
        wsel = sb("wsel", [P, GS, 2 * FF])
        hidA = sb("hidA", [P, FC, GT])
        hidB = sb("hidB", [P, FC, GT])
        cT = glu_a
        gate = hidA
        tok = glu_a[:, :]
        w_out_s = x1T[:, 0:DI]
        w_reduce_s = x1T[:, DI:DI + 2 * HID].rearrange("p (d o) -> p d o", d=2)
        oT = glu_t

        bank_c = [ctx.enter_context(nc.psum_tensor(f"bank_c{i}", [P, GT], F32)) for i in range(2)]
        bank_y = ctx.enter_context(nc.psum_tensor("bank_y", [P, HALVES, GT], F32))
        bank_f = [ctx.enter_context(nc.psum_tensor(f"bank_f{i}", [P, GT], F32)) for i in range(2)]
        bank_k = [ctx.enter_context(nc.psum_tensor(f"bank_k{i}", [P, GT], F32)) for i in range(2)]

        names = """small_loaded front_w_loaded fuse_w_loaded back_w_loaded lora_loaded0 lora_loaded1 base_loaded
            ident_ready pick_zero pick_step consts_ready decay_zero rot_act rot_dve rot_ready a_ready
            hb_ready fused_full fused_ready lora_full lora_merged0 lora_merged1 lora_stored0 lora_stored1
            x_loaded0 x_loaded1 scaled_ready cond_done stats_done aggr_done var_ready rstd_ready xn_ready resid_ready
            front_full taken_f0 taken_f1 conv_init conv_tap u_ready dt_copied rest_ready mid_ready parts_ready
            relu_ready abs_ready exp_ready log_ready delta_ready du_ready
            b_stored0 b_stored1 b_loaded0 b_loaded1 b_loaded2 b_loaded3 c_full exp_done bx_ready scanned product_done states_summed
            y_taken gated_ready back_full taken_k0 taken_k1 y_copied y_turned x1_ready glu_log glu_ready wsel_loaded stored""".split()
        S = namedtuple("Signals", names)(*[sem(n) for n in names])
        x_loaded = (S.x_loaded0, S.x_loaded1)
        b_stored = (S.b_stored0, S.b_stored1)
        b_loaded = (S.b_loaded0, S.b_loaded1, S.b_loaded2, S.b_loaded3)
        taken_f = (S.taken_f0, S.taken_f1)
        taken_k = (S.taken_k0, S.taken_k1)
        lora_loaded = (S.lora_loaded0, S.lora_loaded1)
        lora_merged = (S.lora_merged0, S.lora_merged1)
        lora_stored = (S.lora_stored0, S.lora_stored1)

        def c(name, k=0, p=slice(0, P)):
            return col[p, COLS[name] + k:COLS[name] + k + 1]

        def factors(e):
            room = wsel[0:2 * RANK, 2 * (e % 2):2 * (e % 2) + 2, :].rearrange("r a n -> r (a n)")
            return room[:, 0:HID], room[:, HID:HID + FF], room[:, HID + FF:HID + 2 * FF], room[:, HID + 2 * FF:2 * HID + 2 * FF]

        def staged(e):
            return hidA[:, 2 * (e % 2):2 * (e % 2) + 2, :].rearrange("p a n -> p (a n)")

        base = hidB[:, 0:2, :]

        x_g = x.rearrange("(g s b) (f j) h -> g (b f) s (j h)", s=2, b=2, j=2)
        out_g = out.rearrange("(g b) l h -> g l b h", b=GS)

        def front_at(g, fill):
            return g.number * FRONT_FILLS + (fill + 1)

        def front_taken_at(g, fill):
            return g.number * FRONT_BANK_FILLS[fill % 2] + (fill // 2 + 1)

        def back_at(g, fill):
            return g.number * BACK_FILLS + (fill + 1)

        def taken_at(g, fill):
            return g.number * BANK_FILLS[fill % 2] + (fill // 2 + 1 + 1)

        def unit_at(g, k):
            return g.number * UNITS + (k + 1)

        def around(groups, k):
            j, unit = divmod(k, UNITS)
            return (groups[j], unit) if j in groups else (None, unit)

        def run(eng, period):
            def at(i, c, present):
                period({j: group(i, c + j) for j in present})

            at(0, -1, (1,))
            at(0, 0, (0, 1))
            at(0, 1, (-1, 0, 1))
            with eng.Fori(0, (NG - 4) // 2) as i:
                at(i, 2, (-2, -1, 0, 1))
                at(i, 3, (-2, -1, 0, 1))
            at(0, NG - 2, (-2, -1, 0, 1))
            at(0, NG - 1, (-2, -1, 0))
            at(0, NG, (-2, -1))
            at(0, NG + 1, (-2,))

        def token_order(t):
            return t.rearrange("p (n f j) -> p n f j", n=GS, j=2)

        def transposed_order(t):
            return t.rearrange("p (j n f) -> p n f j", j=2, n=GS)

        block = ctx.enter_context(nc.Block())

        @block.sync
        def _(sp):
            def load_x(g):
                if not (isinstance(g.turn, int) and g.turn == 0):
                    wait(sp, S.cond_done, g.number - 1)
                    wait(sp, S.resid_ready, g.number - 1)
                sp.dma_start(xin[:, g.parity].rearrange("p s j h -> p s (j h)"), x_g[g.number]).then_inc(x_loaded[g.parity], 16)

            def load_selected(g):
                chosen = [sp.value_load(expert_ids[0:1, bass.ds(g.number * GS + s, 1)], min_val=0, max_val=EXPERTS - 1)
                          for s in range(GS)]
                wait(sp, S.back_full, back_at(g, B_WO) - BACK_FILLS)
                for s in range(GS):
                    sp.dma_start(wsel[:, s, :], merged[bass.ds(chosen[s], 1)].rearrange("e p n -> p (e n)")).then_inc(S.wsel_loaded, 16)

            def store(g):
                sp.wait_ge(taken_k[B_TOK % 2], taken_at(g, B_TOK))
                sp.dma_start(out_g[g.number], tok.rearrange("l (b h) -> l b h", b=GS)).then_inc(S.stored, 16)

            def store_b(g, d):
                sp.wait_ge(S.dt_copied, g.number * 2 + (d + 1))
                wait(sp, S.bx_ready, unit_at(g, 16 * d + 15) - UNITS)
                sp.dma_start(b_store[d], dbc[DTR:DTR + NST, :]).then_inc(b_stored[d], 16)

            def load_b(g, k):
                d, n = k // NST, k % NST
                if n == 0:
                    sp.wait_ge(b_stored[d], g.number * 16 + 16)
                else:
                    wait(sp, S.bx_ready, unit_at(g, k) - ROWS + (n == NST - 1))
                sp.dma_start(b_rows[:, k % ROWS], b_store[d, n:n + 1, :].to_broadcast([P, GT])).then_inc(b_loaded[k % ROWS], 16)

            load_x(group(0, 0))
            for b in range(2):
                rows = slice(64 * b, 64 * b + 64)
                sp.dma_start(rot[rows, 0, :], delta_t[b:b + 1, :].to_broadcast([64, BATCH // 2])).then_inc(S.small_loaded, 16)
                sp.dma_start(freq_amp[rows, 0:1], frequencies).then_inc(S.small_loaded, 16)
                sp.dma_start(freq_amp[rows, 1:2], amplitudes).then_inc(S.small_loaded, 16)
            sp.dma_start(col[:, :], columns).then_inc(S.small_loaded, 16)
            sp.dma_start(w_in_s[:, :], w_in).then_inc(S.front_w_loaded, 16)
            sp.dma_start(w_x_s[:, :, :], w_x).then_inc(S.front_w_loaded, 16)
            sp.dma_start(w_dt_s[:, :], w_dt).then_inc(S.front_w_loaded, 16)
            load_x(group(0, 1))
            sp.dma_start(w_out_s, w_out).then_inc(S.fuse_w_loaded, 16)
            sp.dma_start(w_reduce_s, w_reduce).then_inc(S.fuse_w_loaded, 16)
            sp.dma_start(base[:, 0, :], wi).then_inc(S.base_loaded, 16)
            sp.dma_start(base[:, 1, :], wo).then_inc(S.base_loaded, 16)

            def store_merged(e):
                if e < EXPERTS - 1:
                    sp.wait_ge(lora_merged[e % 2], 2 * (e // 2 + 1))
                else:
                    sp.wait_ge(taken_k[0], 1)
                    sp.wait_ge(taken_k[1], 1)
                sp.dma_start(merged[e], staged(e)).then_inc(lora_stored[e % 2] if e < EXPERTS - 1 else S.stored, 16)

            def load_factors(e):
                if e >= 2:
                    sp.wait_ge(S.lora_full, 2 * (e - 1))
                wi_a, wi_b, wo_a, wo_b = factors(e)
                for dst, common, expert in ((wi_a, common_wi_a, experts_wi_a), (wi_b, common_wi_b, experts_wi_b),
                                            (wo_a, common_wo_a, experts_wo_a), (wo_b, common_wo_b, experts_wo_b)):
                    sp.dma_start(dst[0:RANK, :], common).then_inc(lora_loaded[e % 2], 16)
                    sp.dma_start(dst[RANK:2 * RANK, :], expert[e]).then_inc(lora_loaded[e % 2], 16)

            load_factors(0)
            load_factors(1)
            for dst, src in ((w_glu_s[:, :], w_glu), (w1_s[:, :], w1), (w2_s[:, :], w2), (h1_s[:, :, :], h1),
                             (h2_s[:, :, :], h2), (w3_s[:, :, :], w3)):
                sp.dma_start(dst, src).then_inc(S.back_w_loaded, 16)

            def merge(e):
                store_merged(e)
                if e + 2 < EXPERTS:
                    load_factors(e + 2)
                if e == EXPERTS - 1:
                    sp.wait_ge(lora_stored[0], 16 * (EXPERTS // 2))
                    sp.wait_ge(lora_stored[1], 16 * (EXPERTS // 2 - 1))
                    sp.wait_ge(S.stored, 16)

            def period(groups):
                for k in range(UNITS):
                    g, n = around(groups, k + ROW_AHEAD)
                    if g:
                        load_b(g, n)
                    if 0 in groups and -1 not in groups and k in LOADS["merged"]:
                        merge(LOADS["merged"].index(k))
                    for d, j in ((1, 0), (0, 1)):
                        if j in groups and k == LOADS["b_store"][d]:
                            store_b(groups[j], d)
                    if k == LOADS["x"] and 1 in groups and not (isinstance(groups[1].number, int) and groups[1].number < 2):
                        load_x(groups[1])
                    if k == LOADS["store"] and -2 in groups:
                        store(groups[-2])
                    if k == LOADS["selected"] and 0 in groups:
                        load_selected(groups[0])

            run(sp, period)
            sp.wait_ge(S.stored, 16 * (NG + 1))

        @block.gpsimd
        def _(pool):
            nc.gpsimd.memset(ident[:, :], 0.0).then_inc(S.pick_zero, 1)
            pool.wait_ge(S.pick_zero, 1)
            nc.gpsimd.affine_select(out=ident[:, :], in_=ident[:, :], compare_op=ALU.not_equal, fill=1.0, base=0,
                                    pattern=[[-1, P]], channel_multiplier=1).then_inc(S.ident_ready, 1)
            nc.gpsimd.memset(pick[:, :], 0.0).then_inc(S.pick_step, 1)
            for part in range(3):
                pool.wait_ge(S.pick_step, part + 1)
                nc.gpsimd.affine_select(out=pick[:, :], in_=pick[:, :], compare_op=ALU.not_equal, fill=1.0,
                                        base=-32 * part, pattern=[[-1, 32]], channel_multiplier=1).then_inc(S.pick_step, 1)
            nc.gpsimd.memset(half_power[:, :], -0.5).then_inc(S.consts_ready, 1)

            def norm_power(g):
                wait(pool, S.consts_ready, 1)
                wait(pool, S.var_ready, g.number + 1)
                wait(pool, S.xn_ready, g.number)
                nc.gpsimd.tensor_tensor(rstd[:, :], var_eps[:, :], half_power[:, :], ALU.pow).then_inc(S.rstd_ready, 1)

            def residual(g):
                wait(pool, x_loaded[g.parity], g.turn * 16 + 16)
                wait(pool, S.cond_done, g.number + 1)
                wait(pool, S.back_full, back_at(g, B_RES) - 2 * BACK_FILLS)
                nc.gpsimd.tensor_tensor(resid[:, g.parity], xin[:, g.parity].rearrange("p s j h -> p j s h"),
                                        xc[:, :, :, :].rearrange("p s j h -> p j s h"), ALU.add).then_inc(S.resid_ready, 1)

            def step_sizes(g, d):
                wait(pool, S.log_ready, g.number * 2 + (d + 1))
                wait(pool, S.exp_done, unit_at(g, 16 * d + 15) - UNITS)
                nc.gpsimd.tensor_tensor(delta[:, d], relu_dt[:, :, :], log_dt[:, :, :], ALU.add).then_inc(S.delta_ready, 1)

            def inputs(g, d):
                wait(pool, S.delta_ready, g.number * 2 + (d + 1))
                wait(pool, S.u_ready, g.number * 2 + 2)
                wait(pool, S.bx_ready, unit_at(g, 16 * d + 15) - UNITS)
                u = (u_f, u_r)[d]
                nc.gpsimd.tensor_tensor(du[:, d], delta[:, d], u[:, g.parity], ALU.mult).then_inc(S.du_ready, 1)

            def unit(g, k):
                d = k // NST
                if k % NST == 0:
                    pool.wait_ge(S.du_ready, g.number * 2 + (d + 1))
                pool.wait_ge(b_loaded[k % ROWS], g.number * (16 * (UNITS // ROWS)) + 16 * (k // ROWS + 1))
                wait(pool, S.states_summed, unit_at(g, k) - RING)
                nc.gpsimd.tensor_tensor(state[:, k % RING], du[:, d],
                                        b_rows[:, k % ROWS, :].unsqueeze(1).to_broadcast([P, HALVES, GT]),
                                        ALU.mult).then_inc(S.bx_ready, 1)

            def period(groups):
                for k in range(UNITS):
                    g, n = around(groups, k + AHEAD)
                    if g:
                        unit(g, n)
                    for at in (k, k + 0.5):
                        for d, j in ((1, 0), (0, 1)):
                            if j in groups and at == STEPS[d]["delta"]:
                                step_sizes(groups[j], d)
                            if j in groups and at == STEPS[d]["inputs"]:
                                inputs(groups[j], d)
                        if 1 in groups:
                            if at == FRONT["power"]:
                                norm_power(groups[1])
                            if at == FRONT["residual"]:
                                residual(groups[1])

            run(pool, period)

        @block.scalar
        def _(act):
            loaded = []

            def use_table(name):
                if loaded[-1:] != [name]:
                    act.preload_act_table_set(name)
                    loaded.append(name)

            def rotation_tables():
                act.wait_ge(S.small_loaded, 7 * 16)
                act.activation(rot[:, 2, 0:1], freq_amp[:, 1:2], ACT.Ln).then_inc(S.rot_act, 1)
                act.wait_ge(S.rot_act, 1)
                act.activation(rot[:, 3, :], rot[:, 0, :], ACT.Exp, scale=rot[:, 2, 0:1]).then_inc(S.rot_act, 1)
                act.activation(a_neg[:, :, :].rearrange("p h n -> p (h n)"), col[:, COLS["a_log"]:COLS["a_log"] + HALVES * NST],
                               ACT.Exp).then_inc(S.rot_act, 1)
                act.wait_ge(S.rot_dve, 4)
                act.activation(rot[:, 5, :], rot[:, 1, :], ACT.Abs).then_inc(S.rot_act, 1)
                act.wait_ge(S.rot_act, 4)
                act.activation(rot[:, 4, :], rot[:, 1, :], ACT.Sin).then_inc(S.rot_act, 1)
                act.wait_ge(S.consts_ready, 2)
                act.activation(rot[:, 6, :], rot[:, 5, :], ACT.Sin, scale=-1.0, bias=halfpi_col[:, 0:1]).then_inc(S.rot_act, 1)

            def scale_pairs(g):
                wait(act, x_loaded[g.parity], g.turn * 16 + 16)
                wait(act, S.rot_ready, 3)
                wait(act, S.cond_done, g.number)
                for s in range(2):
                    n = bass.ds(g.number * 2 + s, 1)
                    act.activation(scaled[:, s, 0], xin[:, g.parity, s, 0], ACT.Copy, scale=rot[:, 0, n])
                    ins = act.activation(scaled[:, s, 1], xin[:, g.parity, s, 0], ACT.Copy, scale=rot[:, 1, n])
                ins.then_inc(S.scaled_ready, 1)

            def norm_out(g):
                act.wait_ge(S.front_full, front_at(g, F_NORM))
                act.activation(token_order(xnT[:, :]), transposed_order(bank_f[F_NORM % 2][:, :]), ACT.Identity,
                               scale=c("ln_g"), bias=c("ln_b")).then_inc(taken_f[F_NORM % 2], 1)

            def conv_start(g, h):
                act.wait_ge(S.front_full, front_at(g, F_XI0 + h))
                wait(act, S.y_taken, g.number * 2 - 2)
                wait(act, S.u_ready, g.number * 2)
                wait(act, S.delta_ready, g.number * 2)
                tap = c("conv_w", h * TAPS + TAPS - 1)
                bank = bank_f[(F_XI0 + h) % 2]
                act.activation(u_f[:, g.parity, h], bank[:, :], ACT.Identity, scale=tap, bias=c("conv_b", h))
                act.activation(acc_r[:, h], bank[:, :], ACT.Identity, scale=tap, bias=c("conv_b", h)).then_inc(S.conv_init, 1)

            def silu_z(g, h):
                act.wait_ge(S.front_full, front_at(g, F_Z0 + h))
                wait(act, S.gated_ready, g.number * 2 - 2)
                act.activation(z[:, g.parity, h], bank_f[(F_Z0 + h) % 2][:, :], ACT.Silu).then_inc(taken_f[(F_Z0 + h) % 2], 1)

            def silu_u(g):
                act.wait_ge(taken_f[F_XI1 % 2], front_taken_at(g, F_XI1))
                act.activation(u_f[:, g.parity], u_f[:, g.parity], ACT.Silu).then_inc(S.u_ready, 1)
                act.activation(u_r[:, g.parity, :, ::-1], acc_r[:, :, :], ACT.Silu).then_inc(S.u_ready, 1)

            def take_dbc(g, d):
                fill = (F_DBC0, F_DBC1)[d]
                act.wait_ge(S.front_full, front_at(g, fill))
                wait(act, S.c_full, unit_at(g, 16 * d + 15) - UNITS)
                wait(act, b_stored[1 - d], g.number * 16 + 16 * d)
                act.activation(dbc[:, :], bank_f[fill % 2][0:DTR + 2 * NST, :], ACT.Copy)
                act.activation(parts[0:32, d], bank_f[fill % 2][DTR:DTR + 32, :], ACT.Copy).then_inc(S.dt_copied, 1)

            def softplus_in(g, d, h):
                fill = (F_DT00, F_DT10)[d] + h
                act.wait_ge(S.front_full, front_at(g, fill))
                wait(act, S.delta_ready, g.number * 2 + d)
                act.wait_ge(S.u_ready, g.number * 2 + 2)
                act.activation(log_dt[:, h], bank_f[fill % 2][:, :], ACT.Abs, bias=c("dt_b", h)).then_inc(S.abs_ready, 1)
                act.activation(relu_dt[:, h], bank_f[fill % 2][:, :], ACT.Relu, bias=c("dt_b", h)).then_inc(taken_f[fill % 2], 1)

            def softplus_out(g, d):
                use_table(EXP_LN)
                act.wait_ge(S.abs_ready, g.number * 4 + (2 * d + 2))
                act.activation(log_dt[:, :, :], log_dt[:, :, :], ACT.Exp, scale=-1.0).then_inc(S.exp_ready, 1)
                act.wait_ge(S.exp_ready, g.number * 2 + (d + 1))
                act.activation(log_dt[:, :, :], log_dt[:, :, :], ACT.Ln, bias=one_col[:, 0:1]).then_inc(S.log_ready, 1)

            def decays(g, k):
                d, n = k // NST, k % NST
                use_table(EXP_LN)
                if n == 0:
                    act.wait_ge(S.delta_ready, g.number * 2 + (d + 1))
                wait(act, S.scanned, unit_at(g, k) - DECAYS)
                for h in range(HALVES):
                    ins = act.activation(decay[:, k % DECAYS, h, :, 1:], delta[:, d, h].rearrange("p (b t) -> p b t", b=GS)[:, :, 1:],
                                         ACT.Exp, scale=a_neg[:, h, n:n + 1])
                ins.then_inc(S.exp_done, 1)

            def take(g, fill, dst, func, **kw):
                act.wait_ge(S.back_full, back_at(g, fill))
                act.activation(dst, bank_k[fill % 2][:, :], func, **kw).then_inc(taken_k[fill % 2], 1)

            def pair_take(g, pair, fills, dst, func, scale=None):
                for f in (2 * pair, 2 * pair + 1):
                    kw = {} if scale is None else {"scale": c(scale, f)}
                    take(g, fills[f], dst[:, f], func, **kw)

            def back(g, k):
                if k == BACK["out_gelu"]:
                    use_table(GELU)
                    take(g, B_OUT, gy[:, :], ACT.Gelu, bias=c("reduce_b"))
                if k == BACK["glu_taken"]:
                    use_table(EXP_LN)
                    wait(act, S.hb_ready, 1)
                    act.wait_ge(S.stored, g.number * 16 + 16)
                    take(g, B_GLU0, glu_a[:, :], ACT.Identity, bias=c("glu_b", 0))
                    take(g, B_GLU1, glu_t[:, :], ACT.Exp, scale=-1.0, bias=hb[:, 1:2])
                    act.wait_ge(taken_k[B_GLU1 % 2], taken_at(g, B_GLU1))
                    act.activation(glu_t[:, :], glu_t[:, :], ACT.Ln, bias=one_col[:, 0:1]).then_inc(S.glu_log, 1)
                    act.wait_ge(S.glu_log, g.number + 1)
                    act.activation(glu_t[:, :], glu_t[:, :], ACT.Exp, scale=-1.0).then_inc(S.glu_ready, 1)
                if k in BACK["hid_relu"]:
                    pair_take(g, BACK["hid_relu"].index(k), B_HID, hidA, ACT.Relu)
                if k == BACK["wo_taken"]:
                    take(g, B_WO, cT[:, :], ACT.Copy)
                for name, fills, dst, scale in (("h1_gelu", B_H1, hidA, "h1_s"), ("h2_gelu", B_H2, hidB, "h2_s")):
                    if k in BACK[name]:
                        use_table(GELU)
                        pair_take(g, BACK[name].index(k), fills, dst, ACT.Gelu, scale)
                if k == BACK["tok_taken"]:
                    take(g, B_TOK, tok, ACT.Copy)

            def copy_y(g, d):
                act.wait_ge(S.states_summed, unit_at(g, NST * d + NST - 1))
                wait(act, S.gated_ready, g.number * 2 + d)
                act.activation(y_rows[:, :, :], bank_y[:, :, :], ACT.Copy).then_inc(S.y_copied, 1)

            def front(g, k):
                if k == FRONT["scale"]:
                    scale_pairs(g)
                if k == FRONT["norm_taken"]:
                    norm_out(g)
                if k in FRONT["conv_start"]:
                    conv_start(g, FRONT["conv_start"].index(k))

            def steps(g, k, d):
                if k == STEPS[d]["dbc_taken"]:
                    take_dbc(g, d)
                for h in range(HALVES):
                    if k == STEPS[d]["dt_taken"][h]:
                        softplus_in(g, d, h)
                if k == STEPS[d]["softplus"]:
                    softplus_out(g, d)

            def silus(groups):
                use_table(SILU)
                if 1 in groups:
                    silu_z(groups[1], 0)
                if -1 in groups:
                    pair_take(groups[-1], 0, B_GATE, gate, ACT.Silu, "w1_s")
                if 1 in groups:
                    silu_u(groups[1])
                    silu_z(groups[1], 1)
                if -1 in groups:
                    pair_take(groups[-1], 1, B_GATE, gate, ACT.Silu, "w1_s")

            def period(groups):
                for k in range(UNITS):
                    beside(groups, k)
                    g, n = around(groups, k + DECAY_AHEAD)
                    if g:
                        decays(g, n)
                    beside(groups, k + 0.5)

            def beside(groups, k):
                for d in range(2):
                    g, n = around(groups, k - Y["copied"][d])
                    if g and n == 0:
                        copy_y(g, d)
                if 0 in groups:
                    steps(groups[0], k, 1)
                if 1 in groups:
                    front(groups[1], k)
                    steps(groups[1], k, 0)
                if k == SILU_SLOT:
                    silus(groups)
                for j in (-2, -1):
                    if j in groups:
                        back(groups[j], k - j * UNITS)

            rotation_tables()
            act.wait_ge(S.decay_zero, 1)
            act.wait_ge(S.a_ready, 1)
            run(act, period)

        @block.vector
        def _(dve):
            def rotation_tables():
                dve.memset(one_col[:, :], 1.0)
                dve.memset(halfpi_col[:, :], PI / 2).then_inc(S.consts_ready, 1)
                dve.memset(decay[:, :, :, :, :].rearrange("p a h b t -> p (a h b t)"), 0.0).then_inc(S.decay_zero, 1)
                dve.wait_ge(S.small_loaded, 7 * 16)
                dve.tensor_scalar(hb[:, :], col[:, COLS["glu_b"]:COLS["glu_b"] + 2], -1.0, None, ALU.mult).then_inc(S.hb_ready, 1)
                turn_hi = 6.28125
                turn_lo = 2 * PI - turn_hi
                big = 1.5 * 2.0 ** 23
                ang, turns, red = rot[:, 4, :], rot[:, 5, :], rot[:, 1, :]
                dve.tensor_scalar(ang, rot[:, 0, :], freq_amp[:, 0:1], None, ALU.mult).then_inc(S.rot_dve, 1)
                dve.wait_ge(S.rot_dve, 1)
                dve.tensor_scalar(turns, ang, 1.0 / (2 * PI), big, ALU.mult, ALU.add).then_inc(S.rot_ready, 1)
                dve.wait_ge(S.rot_ready, 1)
                dve.tensor_scalar(turns, turns, big, None, ALU.subtract).then_inc(S.rot_dve, 1)
                dve.wait_ge(S.rot_dve, 2)
                dve.scalar_tensor_tensor(rot[:, 7, :], turns, -turn_hi, ang, ALU.mult, ALU.add).then_inc(S.rot_dve, 1)
                dve.wait_ge(S.rot_dve, 3)
                dve.scalar_tensor_tensor(red, turns, -turn_lo, rot[:, 7, :], ALU.mult, ALU.add).then_inc(S.rot_ready, 1)
                dve.wait_ge(S.rot_ready, 2)
                dve.tensor_scalar(red, red, 3.1415925, -3.1415925, ALU.min, ALU.max).then_inc(S.rot_dve, 1)
                dve.wait_ge(S.rot_act, 6)
                dve.tensor_tensor(rot[:, 0, :], rot[:, 3, :], rot[:, 6, :], ALU.mult)
                dve.tensor_tensor(rot[:, 1, :], rot[:, 3, :], rot[:, 4, :], ALU.mult)
                dve.scalar_tensor_tensor(rot[:, 2, :], rot[:, 3, :], -1.0, rot[:, 4, :], ALU.mult, ALU.mult).then_inc(S.rot_ready, 1)
                dve.tensor_scalar(a_neg[:, :, :], a_neg[:, :, :], -1.0, None, ALU.mult).then_inc(S.a_ready, 1)
                dve.wait_ge(S.rot_ready, 3)

            def rotate(g):
                dve.wait_ge(S.scaled_ready, g.number + 1)
                wait(dve, S.resid_ready, g.number)
                wait(dve, S.xn_ready, g.number)
                for s in range(2):
                    n = bass.ds(g.number * 2 + s, 1)
                    x1 = xin[:, g.parity, s, 1]
                    dve.scalar_tensor_tensor(xc[:, s, 0], x1, rot[:, 2, n], scaled[:, s, 0], ALU.mult, ALU.add)
                    ins = dve.scalar_tensor_tensor(xc[:, s, 1], x1, rot[:, 0, n], scaled[:, s, 1], ALU.mult, ALU.add)
                ins.then_inc(S.cond_done, 1)
                dve.wait_ge(S.cond_done, g.number + 1)
                for t in range(GS):
                    ins = dve.bn_stats(stats[:, t], xc[:, t // 2, t % 2])
                ins.then_inc(S.stats_done, 1)
                dve.wait_ge(S.small_loaded, 7 * 16)
                dve.wait_ge(S.stats_done, g.number + 1)
                for t in range(GS):
                    ins = dve.bn_aggr(moments[:, t], stats[:, t])
                ins.then_inc(S.aggr_done, 1)
                dve.wait_ge(S.aggr_done, g.number + 1)
                wait(dve, S.rstd_ready, g.number)
                dve.tensor_scalar(var_eps[:, :], moments[:, :, 1], LN_EPS, None, ALU.add).then_inc(S.var_ready, 1)

            def normalise(g):
                dve.wait_ge(S.rstd_ready, g.number + 1)
                wait(dve, S.front_full, front_at(g, F_NORM) - FRONT_FILLS)
                for t in range(GS):
                    ins = dve.tensor_scalar(xn[:, t // 2, t % 2], xc[:, t // 2, t % 2], moments[:, t, 0:1], rstd[:, t:t + 1],
                                            ALU.subtract, ALU.mult)
                ins.then_inc(S.xn_ready, 1)

            def conv_taps(g, h):
                dve.wait_ge(S.conv_init, g.number * 2 + (h + 1))
                xi = bank_f[(F_XI0 + h) % 2][:, :].rearrange("p (b t) -> p b t", b=GS)
                fwd = u_f[:, g.parity, h].rearrange("p (b t) -> p b t", b=GS)
                rev = acc_r[:, h].rearrange("p (b t) -> p b t", b=GS)
                for m in range(1, TAPS):
                    tap = c("conv_w", h * TAPS + TAPS - 1 - m)
                    if m > 1:
                        dve.wait_ge(S.conv_tap, g.number * 8 + (4 * h + 2 * (m - 1) - 1))
                    ins = dve.scalar_tensor_tensor(fwd[:, :, m:], xi[:, :, :LEN - m], tap, fwd[:, :, m:], ALU.mult, ALU.add)
                    if m < TAPS - 1:
                        ins.then_inc(S.conv_tap, 1)
                        dve.wait_ge(S.conv_tap, g.number * 8 + (4 * h + 2 * (m - 1))) if m > 1 else None
                    else:
                        dve.wait_ge(S.conv_tap, g.number * 8 + (4 * h + 4))
                    ins = dve.scalar_tensor_tensor(rev[:, :, :LEN - m], xi[:, :, m:], tap, rev[:, :, :LEN - m], ALU.mult, ALU.add)
                    ins.then_inc(S.conv_tap if m < TAPS - 1 else taken_f[(F_XI0 + h) % 2], 1)

            def split_rows(g, d):
                dve.wait_ge(S.dt_copied, g.number * 2 + (d + 1))
                fill = (F_DBC0, F_DBC1)[d]
                dve.tensor_tensor(rest[32:64, :], bank_f[fill % 2][DTR:DTR + 32, :], parts[0:32, d],
                                  ALU.subtract).then_inc(taken_f[fill % 2], 1)
                dve.wait_ge(taken_f[fill % 2], front_taken_at(g, fill))
                dve.tensor_copy(parts[32:64, d], rest[32:64, :]).then_inc(S.mid_ready, 1)
                dve.wait_ge(S.mid_ready, g.number * 2 + (d + 1))
                dve.tensor_tensor(parts[64:96, d], rest[32:64, :], parts[32:64, d], ALU.subtract).then_inc(S.parts_ready, 1)

            def unit(g, k):
                dve.wait_ge(S.exp_done, unit_at(g, k))
                dve.wait_ge(S.bx_ready, unit_at(g, k))
                st = state[:, k % RING].rearrange("p h t -> p (h t)")
                dve.tensor_tensor_scan(st, decay[:, k % DECAYS].rearrange("p h b t -> p (h b t)"), st, 0.0,
                                       ALU.mult, ALU.add).then_inc(S.scanned, 1)

            def weigh(g, k):
                dve.wait_ge(S.scanned, unit_at(g, k))
                dve.wait_ge(S.c_full, unit_at(g, k))
                dve.tensor_tensor(state[:, k % RING], state[:, k % RING],
                                  bank_c[k % 2][:, :].unsqueeze(1).to_broadcast([P, HALVES, GT]), ALU.mult).then_inc(S.product_done, 1)

            def take_y(g, d):
                dve.wait_ge(S.y_turned, g.number * 2 + (d + 1))
                wait(dve, S.gated_ready, g.number * 2 + d)
                u = (u_f, u_r)[d]
                for h in range(HALVES):
                    dst = ysum[:, h, :] if d == 0 else ysum[:, h, ::-1]
                    ins = dve.scalar_tensor_tensor(dst, u[:, g.parity, h], c("skip_d", h), bank_y[:, h], ALU.mult, ALU.add)
                ins.then_inc(S.y_taken, 1)
                dve.wait_ge(S.y_taken, g.number * 2 + (d + 1))
                wait(dve, S.back_full, back_at(g, B_OUT) - BACK_FILLS)
                dve.tensor_tensor(gated[:, d], ysum[:, :, :], z[:, g.parity], ALU.mult).then_inc(S.gated_ready, 1)

            def back(g, k):
                if k == BACK["x1"]:
                    dve.wait_ge(taken_k[B_GLU0 % 2], taken_at(g, B_GLU0))
                    dve.wait_ge(S.glu_ready, g.number + 1)
                    dve.tensor_tensor(x1T[:, :], glu_a[:, :], glu_t[:, :], ALU.mult).then_inc(S.x1_ready, 1)
                    dve.wait_ge(S.x1_ready, g.number + 1)
                    dve.wait_ge(S.back_full, back_at(g, B_RES))
                    dve.tensor_tensor(token_order(x1T[:, :]), token_order(x1T[:, :]), transposed_order(bank_k[B_RES % 2][:, :]),
                                      ALU.add).then_inc(taken_k[B_RES % 2], 1)
                if k in BACK["up_taken"]:
                    for j in range(2):
                        f = 2 * BACK["up_taken"].index(k) + j
                        dve.wait_ge(S.back_full, back_at(g, B_UP[f]))
                        dve.wait_ge(taken_k[B_GATE[f] % 2], taken_at(g, B_GATE[f]))
                        dve.scalar_tensor_tensor(hidB[:, f], bank_k[B_UP[f] % 2][:, :], c("w2_s", f), gate[:, f],
                                                 ALU.mult, ALU.mult).then_inc(taken_k[B_UP[f] % 2], 1)
                if k == BACK["w3_taken"]:
                    dve.wait_ge(S.back_full, back_at(g, B_W3))
                    dve.scalar_tensor_tensor(oT[:, :], bank_k[B_W3 % 2][:, :], c("w3_s"), x1T[:, :],
                                             ALU.mult, ALU.add).then_inc(taken_k[B_W3 % 2], 1)

            def merge(e):
                if e == 0:
                    dve.wait_ge(S.base_loaded, 32)
                    dve.wait_ge(S.fused_full, 1)
                    dve.tensor_copy(w_fused[:, :, :, :].rearrange("p d h o -> p (d h o)"), bank_k[0][:, :]).then_inc(S.fused_ready, 1)
                for part in range(2):
                    dve.wait_ge(S.lora_full, 2 * e + part + 1)
                    if e >= 2:
                        dve.wait_ge(lora_stored[e % 2], 16 * (e // 2))
                    dve.scalar_tensor_tensor(staged(e)[:, part * FF:(part + 1) * FF], bank_k[part][:, :], LORA_ALPHA, base[:, part],
                                             ALU.mult, ALU.add).then_inc(lora_merged[e % 2] if e < EXPERTS - 1 else taken_k[part], 1)

            def front(g, k):
                if k == FRONT["rotate"]:
                    rotate(g)
                if k == FRONT["normalise"]:
                    normalise(g)
                if k in FRONT["conv_taps"]:
                    conv_taps(g, FRONT["conv_taps"].index(k))
                if k == STEPS[0]["split"]:
                    split_rows(g, 0)

            def period(groups):
                for k in range(UNITS):
                    if 0 in groups:
                        unit(groups[0], k)
                    beside(groups, k)
                    g, n = around(groups, k - 1)
                    if g:
                        weigh(g, n)
                    beside(groups, k + 0.5)

            def beside(groups, k):
                if 0 in groups and k == STEPS[1]["split"]:
                    split_rows(groups[0], 1)
                for d in range(2):
                    g, n = around(groups, k - Y["taken"][d])
                    if g and n == 0:
                        take_y(g, d)
                if 1 in groups:
                    front(groups[1], k)
                for j in (-2, -1):
                    if j in groups:
                        back(groups[j], k - j * UNITS)
                if 0 in groups and -1 not in groups and k in MERGE_SLOTS:
                    merge(MERGE_SLOTS.index(k))

            rotation_tables()
            run(dve, period)

        @block.tensor
        def _(pe):
            def fill_front(g, fill):
                wait(pe, taken_f[fill % 2], front_taken_at(g, fill) - 1)

            def transpose_norm(g):
                wait(pe, S.ident_ready, 1)
                pe.wait_ge(S.xn_ready, g.number + 1)
                fill_front(g, F_NORM)
                for t in range(GS):
                    s, j = t // 2, t % 2
                    at = (2 * j + s) * P
                    ins = pe.transpose(bank_f[F_NORM % 2][:, at:at + P], xn[:, s, j], ident[:, :])
                ins.then_inc(S.front_full, 1)

            def project_in(g, fill):
                m = fill - F_XI0
                wait(pe, S.front_w_loaded, 48)
                fill_front(g, fill)
                if m == 0:
                    pe.wait_ge(taken_f[F_NORM % 2], front_taken_at(g, F_NORM))
                pe.matmul(bank_f[fill % 2][:, :], w_in_s[:, m * P:(m + 1) * P], xnT[:, :], start=True, stop=True).then_inc(S.front_full, 1)

            def project_x(g, d):
                fill = (F_DBC0, F_DBC1)[d]
                fill_front(g, fill)
                pe.wait_ge(S.u_ready, g.number * 2 + 2)
                u = (u_f, u_r)[d]
                for h in range(HALVES):
                    ins = pe.matmul(bank_f[fill % 2][0:DTR + 2 * NST, :], w_x_s[:, h], u[:, g.parity, h], start=(h == 0), stop=(h == HALVES - 1))
                ins.then_inc(S.front_full, 1)

            def project_dt(g, d, h):
                fill = (F_DT00, F_DT10)[d] + h
                fill_front(g, fill)
                pe.wait_ge(S.dt_copied, g.number * 2 + (d + 1))
                pe.matmul(bank_f[fill % 2][:, :], w_dt_s[:, h * P:(h + 1) * P], dbc[0:DTR, :], start=True, stop=True).then_inc(S.front_full, 1)

            def spread_c(g, k):
                d, n = k // NST, k % NST
                if n == 0:
                    pe.wait_ge(S.parts_ready, g.number * 2 + (d + 1))
                wait(pe, S.product_done, unit_at(g, k) - 2)
                pe.matmul(bank_c[k % 2][:, :], pick[:, NST + n:NST + n + 1].to_broadcast([96, P]), parts[:, d], start=True, stop=True).then_inc(S.c_full, 1)

            def sum_states(g, k):
                d, n = k // NST, k % NST
                pe.wait_ge(S.product_done, unit_at(g, k))
                if n == 0:
                    wait(pe, S.y_taken, g.number * 2 + d)
                for h in range(HALVES):
                    for s in range(GS):
                        ins = pe.matmul(bank_y[:, h, s * P:(s + 1) * P], state[:, k % RING, h, s * LEN:(s + 1) * LEN], ident[:, :],
                                        start=(n == 0 and s == 0), stop=(n == NST - 1), is_transpose=True, skip_group_check=True)
                ins.then_inc(S.states_summed, 1)

            def turn_y(g, d):
                pe.wait_ge(S.y_copied, g.number * 2 + (d + 1))
                for h in range(HALVES):
                    for s in range(GS):
                        ins = pe.transpose(bank_y[:, h, s * LEN:(s + 1) * LEN], y_rows[:, h, s * P:(s + 1) * P], ident[:, :])
                ins.then_inc(S.y_turned, 1)

            def fill_back(g, fill, *sources):
                for bank in range(2):
                    fills = [f for f in (fill - 2, *sources) if f % 2 == bank]
                    if fills:
                        wait(pe, taken_k[bank], taken_at(g, max(fills)))

            def back(g, k):
                if k == BACK["out"]:
                    wait(pe, S.fused_ready, 1)
                    pe.wait_ge(S.gated_ready, g.number * 2 + 2)
                    fill_back(g, B_OUT)
                    for d in range(2):
                        for h in range(HALVES):
                            ins = pe.matmul(bank_k[0][:, :], w_fused[:, d, h], gated[:, d, h], start=(d == 0 and h == 0),
                                            stop=(d == 1 and h == HALVES - 1))
                    ins.then_inc(S.back_full, 1)
                if k == BACK["glu"]:
                    wait(pe, S.back_w_loaded, 6 * 16)
                    for m in range(2):
                        fill_back(g, B_GLU0 + m, B_OUT)
                        pe.matmul(bank_k[(B_GLU0 + m) % 2][:, :], w_glu_s[:, m * P:(m + 1) * P], gy[:, :], start=True,
                                  stop=True).then_inc(S.back_full, 1)
                if k == BACK["residual"]:
                    fill_back(g, B_RES)
                    pe.wait_ge(S.resid_ready, g.number + 1)
                    for t in range(GS):
                        ins = pe.transpose(bank_k[B_RES % 2][:, t * P:(t + 1) * P], resid[:, g.parity, t // 2, t % 2], ident[:, :])
                    ins.then_inc(S.back_full, 1)
                if k in BACK["hid"]:
                    pe.wait_ge(S.wsel_loaded, g.number * (16 * GS) + 16 * GS)
                    for j in range(2):
                        f = 2 * BACK["hid"].index(k) + j
                        fill_back(g, B_HID[f], B_RES)
                        for s in range(GS):
                            ins = pe.matmul(bank_k[f % 2][:, s * LEN:(s + 1) * LEN], wsel[:, s, f * P:(f + 1) * P],
                                            x1T[:, s * LEN:(s + 1) * LEN], start=True, stop=True)
                        ins.then_inc(S.back_full, 1)
                if k == BACK["wo"]:
                    fill_back(g, B_WO, *B_HID)
                    for s in range(GS):
                        for f in range(FC):
                            ins = pe.matmul(bank_k[B_WO % 2][:, s * LEN:(s + 1) * LEN], wsel[:, s, FF + f * HID:FF + (f + 1) * HID],
                                            hidA[:, f, s * LEN:(s + 1) * LEN], start=(f == 0), stop=(f == FC - 1))
                    ins.then_inc(S.back_full, 1)
                for slots, fills, w in ((BACK["gate"], B_GATE, w1_s), (BACK["up"], B_UP, w2_s)):
                    if k in slots:
                        for j in range(2):
                            f = 2 * slots.index(k) + j
                            fill_back(g, fills[f], B_WO)
                            pe.matmul(bank_k[fills[f] % 2][:, :], w[:, f * P:(f + 1) * P], cT[:, :], start=True,
                                      stop=True).then_inc(S.back_full, 1)
                for slots, fills, w, src, before in ((BACK["h1"], B_H1, h1_s, hidB, B_UP), (BACK["h2"], B_H2, h2_s, hidA, B_H1)):
                    if k in slots:
                        f = slots.index(k)
                        fill_back(g, fills[f], *before)
                        for q in range(FC):
                            ins = pe.matmul(bank_k[fills[f] % 2][:, :], w[:, q, f * P:(f + 1) * P], src[:, q],
                                            start=(q == 0), stop=(q == FC - 1))
                        ins.then_inc(S.back_full, 1)
                if k == BACK["w3"]:
                    fill_back(g, B_W3, *B_H2)
                    for q in range(FC):
                        ins = pe.matmul(bank_k[B_W3 % 2][:, :], w3_s[:, q], hidB[:, q], start=(q == 0), stop=(q == FC - 1))
                    ins.then_inc(S.back_full, 1)
                if k == BACK["tok"]:
                    fill_back(g, B_TOK, B_W3)
                    for s in range(GS):
                        ins = pe.transpose(bank_k[B_TOK % 2][:, s * P:(s + 1) * P], oT[:, s * LEN:(s + 1) * LEN], ident[:, :])
                    ins.then_inc(S.back_full, 1)

            def fuse_out():
                pe.wait_ge(S.fuse_w_loaded, 32)
                for d in range(2):
                    for h in range(HALVES):
                        at = (d * HALVES + h) * HID
                        ins = pe.matmul(bank_k[0][:, at:at + HID], w_out_s[:, h * P:(h + 1) * P], w_reduce_s[:, d], start=True, stop=True)
                ins.then_inc(S.fused_full, 1)

            def merge(e):
                wi_a, wi_b, wo_a, wo_b = factors(e)
                pe.wait_ge(lora_loaded[e % 2], 16 * 8 * (e // 2 + 1))
                if e == 0:
                    pe.wait_ge(S.fused_ready, 1)
                else:
                    pe.wait_ge(lora_merged[(e - 1) % 2], 2 * ((e - 1) // 2 + 1))
                pe.matmul(bank_k[0][:, :], wi_a, wi_b, start=True, stop=True).then_inc(S.lora_full, 1)
                for f in range(FC):
                    ins = pe.matmul(bank_k[1][:, f * HID:(f + 1) * HID], wo_a[:, f * P:(f + 1) * P], wo_b, start=True, stop=True)
                ins.then_inc(S.lora_full, 1)

            def front(g, k):
                if k == FRONT["norm"]:
                    transpose_norm(g)
                for slots, fills in ((FRONT["xi"], (F_XI0, F_XI1)), (FRONT["z"], (F_Z0, F_Z1))):
                    if k in slots:
                        project_in(g, fills[slots.index(k)])

            def steps(g, k, d):
                if k == STEPS[d]["dbc"]:
                    project_x(g, d)
                for h in range(HALVES):
                    if k == STEPS[d]["dt"][h]:
                        project_dt(g, d, h)

            def period(groups):
                for k in range(UNITS):
                    g, n = around(groups, k)
                    if g:
                        spread_c(g, n)
                    beside(groups, k)
                    g, n = around(groups, k - SUM_LAG)
                    if g and n % NST >= HELD:
                        for m in range(n - HELD if n % NST == HELD else n, n + 1):
                            sum_states(g, m)
                    beside(groups, k + 0.5)

            def beside(groups, k):
                for d in range(2):
                    g, n = around(groups, k - Y["turned"][d])
                    if g and n == 0:
                        turn_y(g, d)
                if 0 in groups:
                    steps(groups[0], k, 1)
                if 1 in groups:
                    front(groups[1], k)
                    steps(groups[1], k, 0)
                for j in (-2, -1):
                    if j in groups:
                        back(groups[j], k - j * UNITS)
                if 0 in groups and -1 not in groups and k in MERGE_SLOTS:
                    if k == MERGE_SLOTS[0]:
                        fuse_out()
                    merge(MERGE_SLOTS.index(k))

            pe.wait_ge(S.pick_step, 4)
            run(pe, period)


FRONT = {'scale': 4.5, 'rotate': 5.0, 'power': 5.0, 'normalise': 6.5, 'norm': 7.5, 'norm_taken': 9.0, 'xi': (9.0, 10.0), 'conv_start': (10.5, 11.0), 'conv_taps': (10.5, 12.5), 'residual': 13.5, 'z': (14.0, 15.5)}
SILU_SLOT = 17.0
STEPS = ({'dbc': 18.0, 'dbc_taken': 21.0, 'split': 22.5, 'dt': (22.5, 23.0), 'dt_taken': (24.0, 24.0), 'softplus': 24.0, 'delta': 25.5, 'inputs': 26.0}, {'dbc': 0.0, 'dbc_taken': 2.5, 'split': 2.0, 'dt': (3.5, 4.0), 'dt_taken': (5.0, 5.5), 'softplus': 5.5, 'delta': 5.5, 'inputs': 6.5})
LOADS = {'x': 2, 'b_store': (18, 2), 'store': 6, 'selected': 24, 'merged': (8, 10, 12, 14, 16, 18, 20, 22)}
ROW_AHEAD = 5
AHEAD = 3
DECAY_AHEAD = 2
SUM_LAG, HELD = 2, 3
Y = {'copied': (20.0, 36.0), 'turned': (19.5, 36.0), 'taken': (20.5, 36.5)}
BACK = {'out': 37.5, 'out_gelu': 38.5, 'glu': 39.0, 'glu_taken': 39.5, 'residual': 40.5, 'x1': 41.5, 'hid': (42.5, 43.0), 'hid_relu': (42.5, 45.5), 'wo': 45.0, 'wo_taken': 47.0, 'gate': (47.0, 48.0), 'up': (49.5, 50.5), 'up_taken': (51.0, 51.5), 'h1': (52.0, 53.0, 55.5, 56.0), 'h1_gelu': (55.0, 57.0), 'h2': (57.5, 59.0, 62.5, 65.0), 'h2_gelu': (63.0, 67.0), 'w3': 67.0, 'w3_taken': 68.0, 'tok': 68.5, 'tok_taken': 70.0}
MERGE_SLOTS = tuple(k + 0.5 for k in range(6, 6 + 2 * EXPERTS, 2))


def kernel(**inputs):
    import concourse.bacc as _bacc
    from concourse.bass_utils import run_bass_kernel_spmd as _run

    def host(name):
        return np.asarray(inputs[name])

    def halves(a):
        return a.reshape(HALVES, P, -1).transpose(1, 0, 2).reshape(P, -1)

    def chunked(a):
        return a.reshape(-1, P, a.shape[1]).transpose(1, 0, 2)

    attn, cond2, ffn = "L0_attn_", "L0_cond2_", "L0_ffn_"
    columns = np.concatenate([
        halves(host(attn + "conv_w").reshape(DI, TAPS)), halves(host(attn + "conv_b")), halves(host(attn + "dt_proj_b")),
        halves(host(attn + "D")), halves(host(attn + "A_log")), host(attn + "ln_g").reshape(P, 1), host(attn + "ln_b").reshape(P, 1),
        host(attn + "dim_reduce_b").reshape(P, 1), halves(host(attn + "glu_b")),
        host(ffn + "w1_s").reshape(FC, P).T, host(ffn + "w2_s").reshape(FC, P).T, host(ffn + "h1_s").reshape(FC, P).T,
        host(ffn + "h2_s").reshape(FC, P).T, host(ffn + "w3_s").reshape(P, 1)], axis=1)
    arrays = {
        "x": host("x"), "delta_t": host("condB_deltat").reshape(BATCH // 2, 2).T, "expert_ids": host("itok_B_0_7").reshape(1, BATCH),
        "amplitudes": host("L0_cond_amplitudes").reshape(-1, 1), "frequencies": host("L0_cond_frequencies").reshape(-1, 1),
        "columns": columns,
        "w_in": host(attn + "in_proj_w").T, "w_x": chunked(host(attn + "x_proj_w").T), "w_dt": host(attn + "dt_proj_w").T,
        "w_out": host(attn + "out_proj_w"), "w_reduce": chunked(host(attn + "dim_reduce_w").T), "w_glu": host(attn + "glu_w").T,
        "wi": host(cond2 + "wi").T, "wo": chunked(host(cond2 + "wo").T).reshape(P, FF),
        "common_wi_a": host(cond2 + "common_wi_a"), "common_wi_b": host(cond2 + "common_wi_b").T,
        "common_wo_a": host(cond2 + "common_wo_a"), "common_wo_b": host(cond2 + "common_wo_b").T,
        "experts_wi_a": host(cond2 + "experts_wi_a"), "experts_wi_b": host(cond2 + "experts_wi_b").transpose(0, 2, 1),
        "experts_wo_a": host(cond2 + "experts_wo_a"), "experts_wo_b": host(cond2 + "experts_wo_b").transpose(0, 2, 1),
        "w1": host(ffn + "w1_w").T, "w2": host(ffn + "w2_w").T, "h1": chunked(host(ffn + "h1_w").T),
        "h2": chunked(host(ffn + "h2_w").T), "w3": chunked(host(ffn + "w3_w").T),
    }
    arrays = {f"in_{k}": np.ascontiguousarray(v) for k, v in arrays.items()}
    nc = _bacc.Bacc("TRN2", target_bir_lowering=False, num_devices=1)
    args = [nc.dram_tensor(k, v.shape, mybir.dt.from_np(v.dtype), kind="ExternalInput").ap() for k, v in arrays.items()]
    args.append(nc.dram_tensor("merged", (EXPERTS, P, 2 * FF), F32, kind="Internal").ap())
    args.append(nc.dram_tensor("b_store", (2, NST, GT), F32, kind="Internal").ap())
    args.append(nc.dram_tensor("out", (BATCH, LEN, HID), F32, kind="ExternalOutput").ap())
    build(nc, *args)
    r = _run(nc, [arrays], core_ids=[0])
    return r.results[0]["out"]
```
